# Optimizing a Trainium2 kernel written in Bass

```python
import numpy as np
import jax
import jax.numpy as jnp

def _softmax(x, axis=-1):
    return jax.nn.softmax(x, axis=axis)

def _gelu(x):
    return jax.nn.gelu(x, approximate=True)

def _silu(x):
    return jax.nn.silu(x)

def _sigmoid(x):
    return jax.nn.sigmoid(x)

def _layernorm(x, axis=-1, eps=1e-05):
    m = jnp.mean(x, axis=axis, keepdims=True)
    v = jnp.var(x, axis=axis, keepdims=True)
    return (x - m) / jnp.sqrt(v + eps)

def _scatter_add(tgt, idx, src, axis=0):
    return tgt.at[idx].add(src)

def _segment_sum(src, seg, n):
    return jax.ops.segment_sum(src, seg, n)
kernel_name = 'mk_flamingo_gated_d1_seqx_r8_66e871'

def setup_inputs(seed: int=0):
    np.random.seed(seed)
    _w = jnp.asarray

    def _rec_inputs():
        import jax
        import jax.numpy as jnp
        _rk = jax.random.key(seed)
        x = -0.0002928 + 1 * jax.random.normal(jax.random.fold_in(_rk, 1), (8, 256, 128), jnp.float32)
        _lenS = 256 - jax.random.randint(jax.random.fold_in(_rk, 7), (8,), 0, max(1, 256 // 4) + 1, jnp.int32)
        _lenS2 = 64 - jax.random.randint(jax.random.fold_in(_rk, 8), (8,), 0, max(1, 64 // 4) + 1, jnp.int32)
        _ctx_1024P = jax.random.normal(jax.random.fold_in(_rk, 11), (8, 16, 128), jnp.float32)
        _ctx_1024c = jax.random.dirichlet(jax.random.fold_in(_rk, 511), 0.3 * jnp.ones((16,), jnp.float32), (8, 64))
        _ctx_1024t = jnp.einsum('bsk,bkd->bsd', _ctx_1024c, _ctx_1024P)
        _ctx_1024t = _ctx_1024t * jax.lax.rsqrt(jnp.mean(jnp.square(_ctx_1024t)) + 1e-12) * 0.953939
        ctx_1024 = -1.39393e-06 + 0.999914 * (_ctx_1024t + 0.3 * jax.random.normal(jax.random.fold_in(_rk, 611), (8, 64, 128), jnp.float32))
        _g = jax.random.normal(jax.random.fold_in(_rk, 9001), (2, 1), jnp.float32)
        _g = jnp.sign(_g) * jnp.maximum(jnp.abs(_g), 1.0) + (_g == 0) * 1.0
        g_xattn = _g[0]
        g_ffn = _g[1]
        return (x, ctx_1024, g_xattn, g_ffn)
    x, ctx_1024, g_xattn, g_ffn = _rec_inputs()

    def _L0_xattn_setup():
        import jax, jax.numpy as jnp
        import numpy as np
        import math
        D_MODEL = 128
        N_HEADS = 16
        HEAD_DIM = D_MODEL // N_HEADS
        TOP_K = 32
        SCALE = math.sqrt(HEAD_DIM)

        def _split_heads(t, n):
            B, L, _ = t.shape
            return t.reshape(B, L, N_HEADS, HEAD_DIM).transpose(0, 2, 1, 3)
        key = jax.random.key(seed)
        ks = jax.random.split(key, 12)
        B, S, N = (2, 256, 256)
        std = 1.0 / math.sqrt(D_MODEL)
        inp = {'x': jax.random.normal(ks[0], (B, S, D_MODEL), dtype=jnp.float32), 'knowledge_embeddings': jax.random.normal(ks[1], (B, N, D_MODEL), dtype=jnp.float32), 'Wq': jax.random.normal(ks[2], (D_MODEL, D_MODEL), dtype=jnp.float32) * std, 'bq': jnp.zeros((D_MODEL,), dtype=jnp.float32), 'Wk': jax.random.normal(ks[3], (D_MODEL, D_MODEL), dtype=jnp.float32) * std, 'bk': jnp.zeros((D_MODEL,), dtype=jnp.float32), 'Wv': jax.random.normal(ks[4], (D_MODEL, D_MODEL), dtype=jnp.float32) * std, 'bv': jnp.zeros((D_MODEL,), dtype=jnp.float32), 'Wo': jax.random.normal(ks[5], (D_MODEL, D_MODEL), dtype=jnp.float32) * std, 'bo': jnp.zeros((D_MODEL,), dtype=jnp.float32)}
        return inp
    _L0_xattn_all = _L0_xattn_setup()
    _L0_xattn_in = {k: v for k, v in _L0_xattn_all.items() if k in ('Wq', 'bq', 'Wk', 'bk', 'Wv', 'bv', 'Wo', 'bo')}
    del _L0_xattn_all

    def _L0_ffn_setup():
        import jax, jax.numpy as jnp
        import numpy as np
        B, S, H, F, E = (2, 256, 128, 512, 8)
        key = jax.random.key(seed)
        ks = jax.random.split(key, 4)
        x = jax.random.normal(ks[0], (B, S, H), dtype=jnp.float32)
        w_router = jax.random.normal(ks[1], (H, E), dtype=jnp.float32) * 0.02
        w1 = jax.random.normal(ks[2], (E, H, F), dtype=jnp.float32) * 0.02
        b1 = jnp.zeros((E, F), dtype=jnp.float32)
        w2 = jax.random.normal(ks[3], (E, F, H), dtype=jnp.float32) * 0.02
        b2 = jnp.zeros((E, H), dtype=jnp.float32)
        return {'x': x, 'w_router': w_router, 'w1': w1, 'b1': b1, 'w2': w2, 'b2': b2}
    _L0_ffn_all = _L0_ffn_setup()
    _L0_ffn_in = {k: v for k, v in _L0_ffn_all.items() if k in ('w_router', 'w1', 'b1', 'w2', 'b2')}
    del _L0_ffn_all
    return {'x': x, 'ctx_1024': ctx_1024, 'g_xattn': g_xattn, 'g_ffn': g_ffn, 'L0_xattn_Wq': _L0_xattn_in['Wq'], 'L0_xattn_bq': _L0_xattn_in['bq'], 'L0_xattn_Wk': _L0_xattn_in['Wk'], 'L0_xattn_bk': _L0_xattn_in['bk'], 'L0_xattn_Wv': _L0_xattn_in['Wv'], 'L0_xattn_bv': _L0_xattn_in['bv'], 'L0_xattn_Wo': _L0_xattn_in['Wo'], 'L0_xattn_bo': _L0_xattn_in['bo'], 'L0_ffn_w_router': _L0_ffn_in['w_router'], 'L0_ffn_w1': _L0_ffn_in['w1'], 'L0_ffn_b1': _L0_ffn_in['b1'], 'L0_ffn_w2': _L0_ffn_in['w2'], 'L0_ffn_b2': _L0_ffn_in['b2']}

def reference(x, ctx_1024, g_xattn, g_ffn, L0_xattn_Wq, L0_xattn_bq, L0_xattn_Wk, L0_xattn_bk, L0_xattn_Wv, L0_xattn_bv, L0_xattn_Wo, L0_xattn_bo, L0_ffn_w_router, L0_ffn_w1, L0_ffn_b1, L0_ffn_w2, L0_ffn_b2):
    import jax
    import jax.numpy as jnp

    def _L0_xattn_ref(x, knowledge_embeddings, Wq, bq, Wk, bk, Wv, bv, Wo, bo):
        import jax, jax.numpy as jnp
        import numpy as np
        import math
        D_MODEL = 128
        N_HEADS = 16
        HEAD_DIM = D_MODEL // N_HEADS
        TOP_K = 32
        SCALE = math.sqrt(HEAD_DIM)

        def _split_heads(t, n):
            B, L, _ = t.shape
            return t.reshape(B, L, N_HEADS, HEAD_DIM).transpose(0, 2, 1, 3)
        B, S, _ = x.shape
        N = knowledge_embeddings.shape[1]
        Q = _split_heads(x @ Wq.T + bq, N_HEADS)
        K = _split_heads(knowledge_embeddings @ Wk.T + bk, N_HEADS)
        V = _split_heads(knowledge_embeddings @ Wv.T + bv, N_HEADS)
        scores = jnp.einsum('bhsd,bhnd->bhsn', Q, K) / SCALE
        k = min(TOP_K, N)
        topk_scores, topk_indices = jax.lax.top_k(scores, k)
        sparse_weights = jax.nn.softmax(topk_scores, axis=-1)
        sel_V = jnp.take_along_axis(V[:, :, None, :, :], topk_indices[..., None], axis=3)
        context = jnp.einsum('bhsk,bhskd->bhsd', sparse_weights, sel_V)
        context = context.transpose(0, 2, 1, 3).reshape(B, S, D_MODEL)
        return context @ Wo.T + bo

    def _L0_ffn_ref(x, w_router, w1, b1, w2, b2):
        import jax, jax.numpy as jnp
        import numpy as np
        B, S, H, F, E = (2, 256, 128, 512, 8)
        'Top-1 MoE layer: route -> per-expert FFN -> weighted combine.\n\n            Faithful to ExpertParallelWrapper._process_moe_layer on a single group:\n            router picks one expert per token with a routing weight; tokens are\n            dispatched to experts (here expressed as a static mask over the fixed\n            expert set), processed by the expert FFN, and scatter-combined back\n            weighted by the routing probability.\n            '
        Bs, Ss, Hs = x.shape
        n_experts = w1.shape[0]
        logits = jnp.einsum('bsh,he->bse', x, w_router)
        probs = jax.nn.softmax(logits, axis=-1)
        sel = jnp.argmax(probs, axis=-1)
        wgt = jnp.take_along_axis(probs, sel[..., None], axis=-1)[..., 0]
        xt = x.reshape(-1, Hs)
        sel_t = sel.reshape(-1)
        wgt_t = wgt.reshape(-1)
        out = jnp.zeros_like(xt)
        for e in range(n_experts):
            h = jax.nn.relu(xt @ w1[e] + b1[e])
            y = h @ w2[e] + b2[e]
            m = (sel_t == e).astype(xt.dtype) * wgt_t
            out = out + m[:, None] * y
        return out.reshape(Bs, Ss, Hs)
    x = x + jnp.tanh(g_xattn[0]) * _L0_xattn_ref(_layernorm(x, axis=-1), ctx_1024, L0_xattn_Wq, L0_xattn_bq, L0_xattn_Wk, L0_xattn_bk, L0_xattn_Wv, L0_xattn_bv, L0_xattn_Wo, L0_xattn_bo)
    x = x + jnp.tanh(g_ffn[0]) * _L0_ffn_ref(_layernorm(x, axis=-1), L0_ffn_w_router, L0_ffn_w1, L0_ffn_b1, L0_ffn_w2, L0_ffn_b2)
    return x

_drawn_inputs = setup_inputs


def setup_inputs(seed=0):
    import zlib

    import numpy as np

    out = dict(_drawn_inputs(seed))
    spreads = {'L0_xattn_bq': (0.0, 0.271),
     'L0_xattn_bk': (0.0, 0.8),
     'L0_xattn_bv': (0.0, 0.1),
     'L0_xattn_bo': (0.0, 0.1),
     'L0_ffn_b1': (0.0, 0.8),
     'L0_ffn_b2': (0.0, 0.554)}
    factors = {'L0_ffn_w_router': 3.279, 'L0_ffn_w1': 6.272, 'L0_ffn_w2': 4.873}
    for name, (base, spread) in spreads.items():
        noise = np.random.default_rng([zlib.crc32(name.encode()), seed]).standard_normal(out[name].shape)
        drawn = base * np.exp(spread * noise) if base else spread * noise
        out[name] = jnp.asarray(drawn.astype(out[name].dtype))
    for name, factor in factors.items():
        out[name] = (out[name] * factor).astype(out[name].dtype)
    return out
```

```python
import concourse.bass as bass
import numpy as np
from concourse import mybir
from contextlib import ExitStack

F32 = mybir.dt.float32
U32 = mybir.dt.uint32
ALU = mybir.AluOpType
ACT = mybir.ActivationFunctionType

P = 128
B, S, D = 8, 256, 128
N = 64
HEADS = 16
HD = D // HEADS
TOPK = 32
E_N = 8
F = 512
FC = F // P
TILES = B * S // P
PAIRS = HEADS // 2
VW = 2 * HD + 2
SCALE = float(HD) ** -0.5
NEG = -3.0e38
EPS = 1e-5

C_ID, C_HM, C_IOTA = 0, 128, 144
C_W = 152
LOOP_FROM, LOOP_TO = 4, 14


def build(nc, t):
    ctx = ExitStack()
    with ctx:
        def sb(name, shape, dt=F32):
            return ctx.enter_context(nc.sbuf_tensor(name, shape, dt))

        def ps(name, shape):
            return ctx.enter_context(nc.psum_tensor(name, shape, F32))

        def sem(name):
            return ctx.enter_context(nc.semaphore(name))

        x_all = sb("x_all", [P, TILES, D])
        const = sb("const", [P, C_W])
        ident = const[:, C_ID:C_ID + P]
        head_mask = const[:, C_HM:C_HM + HEADS]
        iota8 = const[:, C_IOTA:C_IOTA + E_N]
        ones_row = sb("ones_row", [1, P])
        half_neg = sb("half_neg", [P, 1])
        wq = sb("wq", [P, D])
        wk = sb("wk", [P, D])
        wv = sb("wv", [P, D])
        wo = sb("wo", [P, D])
        wr = sb("wr", [P, E_N])
        ctx_t = sb("ctx_t", [P, B, 2, N])
        bq = sb("bq", [P, 1])
        bk = sb("bk", [P, 1])
        bv_row = sb("bv_row", [1, D])
        bo_row = sb("bo_row", [1, D])
        b2_row = sb("b2_row", [1, E_N * D])
        b1_t = sb("b1_t", [P, E_N * FC])
        gates = sb("gates", [P, 2])
        tg = sb("tg", [P, 2])
        w1 = sb("w1", [P, E_N, F])
        w2 = sb("w2", [P, E_N, FC, D])
        k_t = sb("k_t", [P, B, N])
        kb = sb("kb", [P, B, HEADS, N])
        vb = sb("vb", [P, B, PAIRS, VW])
        stats = sb("stats", [P, 2, 6])
        mv = sb("mv", [P, 2, 2])
        rstd = sb("rstd", [P, 2, 3])
        xn = sb("xn", [P, 2, D])
        xn_t = sb("xn_t", [P, 2, P])
        q_t = sb("q_t", [P, 2, P])
        s_sb = sb("s_sb", [P, 2, HEADS, N])
        work = sb("work", [P, HEADS, N])
        v8 = sb("v8", [P, 2, HEADS, 8])
        vr = sb("vr", [P, 2, HEADS, 8])
        d_sb = sb("d_sb", [P, HEADS, N])
        e_sb = sb("e_sb", [P, HEADS, N])
        p_sb = sb("p_sb", [P, 2, PAIRS, P])
        p_t = sb("p_t", [P, PAIRS, P])
        rden = sb("rden", [P, HEADS])
        cn = sb("cn", [P, D])
        c_t = sb("c_t", [P, P])
        x1 = sb("x1", [P, 2, D])
        stats2 = sb("stats2", [P, 6])
        mv2 = sb("mv2", [P, 2])
        rstd2 = sb("rstd2", [P, 3])
        xn2 = sb("xn2", [P, D])
        xn2_t = sb("xn2_t", [P, 2, P])
        top8 = sb("top8", [P, 8])
        idx8 = sb("idx8", [P, 8], U32)
        idxf = sb("idxf", [P, 1])
        dl = sb("dl", [P, 8])
        el = sb("el", [P, 8])
        esum = sb("esum", [P, 1])
        wgt = sb("wgt", [P, 2])
        route = sb("route", [P, 2, E_N])
        h_t = sb("h_t", [P, 2, FC, P])

        ps_s = ps("ps_s", [P, HEADS, N])
        ps_p = ps_s[:].rearrange("p (j h) n -> p j (h n)", h=2)
        ps_h = [ps(f"ps_h{i}", [P, FC, P]) for i in range(2)]
        ps_y = [ps(f"ps_y{i}", [P, 512])[:, 0:D] for i in range(2)]
        ps_front = ps("ps_front", [P, 512])
        ps_xt, ps_q = ps_front[:, 0:128], ps_front[:, 128:256]
        ps_att = ps("ps_att", [P, 512])
        ps_pv = ps_att[:, 0:PAIRS * VW].rearrange("p (j v) -> p j v", v=VW)
        ps_c = ps_x2 = ps_att[:, 144:272]
        ps_o = ps_att[:, 272:400]
        ps_l = ps_att[:, 400:408]

        x_first, x_rest = sem("x_first"), sem("x_rest")
        w_q, w_kv, w_late, w_moe, consts_in = sem("w_q"), sem("w_kv"), sem("w_late"), sem("w_moe"), sem("consts_in")
        consts_set, gate_ready = sem("consts_set"), sem("gate_ready")
        k_mm, k_ready, kb_zero, kb_ready = sem("k_mm"), sem("k_ready"), sem("kb_zero"), sem("kb_ready")
        v_mm, vb_zero, v_ready = sem("v_mm"), sem("vb_zero"), sem("v_ready")
        st1_raw, st1, var1, rsq1, r1 = sem("st1_raw"), sem("st1"), sem("var1"), sem("rsq1"), sem("r1")
        xn_ready, xt_mm, xt_ready, q_mm, q_ready = sem("xn_ready"), sem("xt_mm"), sem("xt_ready"), sem("q_mm"), sem("q_ready")
        s_mm, s_ready = sem("s_mm"), sem("s_ready")
        found, removed = sem("found"), sem("removed")
        d_ready, e_ready, p_ready, p_mm, pt_ready = sem("d_ready"), sem("e_ready"), sem("p_ready"), sem("p_mm"), sem("pt_ready")
        pv_mm, rden_ready, cn_ready, c_mm, ct_ready, o_mm = sem("pv_mm"), sem("rden_ready"), sem("cn_ready"), sem("c_mm"), sem("ct_ready"), sem("o_mm")
        x1_ready = sem("x1_ready")
        st2_raw, st2, var2, rsq2, r2 = sem("st2_raw"), sem("st2"), sem("var2"), sem("rsq2"), sem("r2")
        xn2_ready, x2_mm, x2_ready, l_mm = sem("xn2_ready"), sem("x2_mm"), sem("x2_ready"), sem("l_mm")
        top_ready, dl_ready, el_ready, idx_ready = sem("top_ready"), sem("dl_ready"), sem("el_ready"), sem("idx_ready")
        wgt_a, wgt_b, route_ready = sem("wgt_a"), sem("wgt_b"), sem("route_ready")
        h_mm, h_ready, y_mm, acc_done, stored = sem("h_mm"), sem("h_ready"), sem("y_mm"), sem("acc_done"), sem("stored")

        block = ctx.enter_context(nc.Block())

        def run(step_of, first, last):
            def go(eng):
                for k in range(first, LOOP_FROM):
                    step_of(k, k % 2, k)
                with eng.Fori(LOOP_FROM // 2, LOOP_TO // 2) as i:
                    step_of(i * 2, 0, None)
                    step_of(i * 2 + 1, 1, None)
                for k in range(LOOP_TO, last):
                    step_of(k, k % 2, k)
            return go

        def has(k, lag):
            return k is None or 0 <= k - lag < TILES

        def later(k, lag, n):
            return k is None or k - lag >= n


        @block.sync
        def _(sp):
            sp.dma_start(x_all[:, 0:2, :], t["x"][:, 0:2, :]).then_inc(x_first, 16)
            sp.dma_start(const[:], t["const"]).then_inc(consts_in, 16)
            sp.dma_start(wq[:], t["wq"]).then_inc(w_q, 16)
            sp.dma_start(bq[:], t["bq"]).then_inc(w_q, 16)
            sp.dma_start(x_all[:, 2:TILES, :], t["x"][:, 2:TILES, :]).then_inc(x_rest, 16)
            sp.dma_start(w1[:], t["w1"]).then_inc(w_moe, 16)
            sp.dma_start(b1_t[:], t["b1"]).then_inc(w_moe, 16)

            def step(k, par, kk):
                if has(kk, 2):
                    sp.wait_ge(acc_done, (k - 2) * E_N + E_N)
                    sp.dma_start(t["out"][:, bass.ds(k - 2, 1), :], x1[:, par:par + 1, :]).then_inc(stored, 16)
            run(step, 2, TILES + 2)(sp)
            sp.wait_ge(stored, 16 * TILES)

        @block.gpsimd
        def _(pool):
            nc.gpsimd.memset(ones_row[:], 1.0).then_inc(consts_set, 1)
            nc.gpsimd.memset(half_neg[:], -0.5).then_inc(consts_set, 1)
            nc.gpsimd.memset(vb[:], 0.0).then_inc(vb_zero, 1)
            pool.wait_ge(vb_zero, 1)
            nc.gpsimd.memset(vb[0:64, :, :, 2 * HD:2 * HD + 1], 1.0).then_inc(vb_zero, 1)
            nc.gpsimd.memset(vb[64:128, :, :, 2 * HD + 1:VW], 1.0).then_inc(vb_zero, 1)
            pool.wait_ge(consts_in, 16)
            pool.wait_ge(consts_set, 2)
            pool.wait_ge(vb_zero, 3)

            def rsqrt(st_sem, var_sem, rsq_sem, r_sem, mv_, r_, n):
                pool.wait_ge(st_sem, n + 1)
                pool.nop(nofuse=True)
                nc.gpsimd.tensor_scalar(r_[:, 2:3], mv_[:, 1:2], EPS, None, ALU.add).then_inc(var_sem, 1)
                pool.wait_ge(var_sem, n + 1)
                nc.gpsimd.tensor_tensor(r_[:, 0:1], r_[:, 2:3], half_neg[:], ALU.pow).then_inc(rsq_sem, 1)
                pool.wait_ge(rsq_sem, n + 1)
                pool.nop(nofuse=True)
                nc.gpsimd.tensor_scalar(r_[:, 1:2], mv_[:, 0:1], r_[:, 0:1], -1.0, ALU.mult, ALU.mult).then_inc(r_sem, 1)

            def spread_keys(b):
                nc.gpsimd.tensor_tensor(kb[:, b, :, :], k_t[:, b, :].unsqueeze(1).to_broadcast([P, HEADS, N]),
                                        head_mask.unsqueeze(2).to_broadcast([P, HEADS, N]),
                                        ALU.mult).then_inc(kb_ready, 1)

            def step(k, par, kk):
                if has(kk, -2):
                    rsqrt(st1, var1, rsq1, r1, mv[:, par, :], rstd[:, par, :], k + 2)
                if kk == -2:
                    pool.wait_ge(k_ready, 1)
                    for b in range(B):
                        spread_keys(b)
                if has(kk, 0):
                    pool.wait_ge(found, k * 8 + 2)
                    if later(kk, 0, 1):
                        pool.wait_ge(e_ready, k)
                    nc.gpsimd.tensor_tensor(d_sb[:], s_sb[:, par], v8[:, par, :, 0:1].to_broadcast([P, HEADS, N]),
                                            ALU.subtract).then_inc(d_ready, 1)
                if has(kk, 1):
                    rsqrt(st2, var2, rsq2, r2, mv2[:], rstd2[:], k - 1)
            run(step, -2, TILES + 1)(pool)

        @block.scalar
        def _(act):
            act.dma_start(wk[:], t["wk"]).then_inc(w_kv, 16)
            act.dma_start(ctx_t[:], t["ctx"]).then_inc(w_kv, 16)
            act.dma_start(bk[:], t["bk"]).then_inc(w_kv, 16)
            act.dma_start(wv[:], t["wv"]).then_inc(w_kv, 16)
            act.dma_start(bv_row[:], t["bv"]).then_inc(w_kv, 16)
            act.dma_start(gates[:], t["gates"]).then_inc(w_late, 16)
            act.dma_start(wo[:], t["wo"]).then_inc(w_late, 16)
            act.dma_start(bo_row[:], t["bo"]).then_inc(w_late, 16)
            act.dma_start(wr[:], t["wr"]).then_inc(w_late, 16)
            act.dma_start(w2[:], t["w2"]).then_inc(w_moe, 16)
            act.dma_start(b2_row[:], t["b2"]).then_inc(w_moe, 16)

            def norm(xin, r_, out, r_sem, n, out_sem):
                act.wait_ge(r_sem, n + 1)
                nc.scalar.activation(out, xin, ACT.Identity, scale=r_[:, 0:1], bias=r_[:, 1:2]).then_inc(out_sem, 1)

            def experts(k, par, kk, e):
                if not has(kk, 2):
                    return
                n = (k - 2) * E_N + e
                if kk is None or kk > 2 or e >= 2:
                    act.wait_ge(y_mm, n - 1)
                act.wait_ge(h_mm, n + 1)
                if e == 0 and kk == 2:
                    act.wait_ge(w_moe, 64)
                for c in range(FC):
                    last = nc.scalar.activation(h_t[:, e % 2, c, :], ps_h[e % 2][:, c, :], ACT.Relu,
                                                bias=b1_t[:, e * FC + c:e * FC + c + 1])
                last.then_inc(h_ready, 1)

            def front(k, par, kk):
                if not has(kk, -2):
                    return
                f = k + 2
                norm(x_all[:, bass.ds(f, 1), :], rstd[:, par, :], xn[:, par, :], r1, f, xn_ready)
                act.wait_ge(xt_mm, f + 1)
                nc.scalar.activation(xn_t[:, par, :], ps_xt, ACT.Copy).then_inc(xt_ready, 1)
                if kk == -2:
                    act.wait_ge(w_q, 32)
                act.wait_ge(q_mm, f + 1)
                nc.scalar.activation(q_t[:, par, :], ps_q, ACT.Identity, bias=bq[:]).then_inc(q_ready, 1)

            def step(k, par, kk):
                nxt = (par + 1) % 2
                if has(kk, 1):
                    act.wait_ge(p_mm, k)
                    if later(kk, 1, 1):
                        act.wait_ge(pv_mm, k - 1)
                    nc.scalar.activation(p_t[:], ps_p[:], ACT.Copy).then_inc(pt_ready, 1)
                experts(k, par, kk, 0)
                experts(k, par, kk, 1)
                if has(kk, -1):
                    act.wait_ge(s_mm, k + 2)
                    if later(kk, -1, 2):
                        act.wait_ge(d_ready, k)
                        act.wait_ge(removed, (k - 1) * 8 + 2)
                    nc.scalar.activation(s_sb[:, nxt], ps_s[:], ACT.Copy).then_inc(s_ready, 1)
                experts(k, par, kk, 2)
                if has(kk, 0):
                    act.wait_ge(d_ready, k + 1)
                    if later(kk, 0, 1):
                        act.wait_ge(p_ready, k)
                    nc.scalar.activation(e_sb[:], d_sb[:], ACT.Exp, scale=SCALE).then_inc(e_ready, 1)
                experts(k, par, kk, 3)
                if has(kk, 1):
                    act.wait_ge(c_mm, k)
                    if later(kk, 1, 1):
                        act.wait_ge(o_mm, k - 1)
                    nc.scalar.activation(c_t[:], ps_c, ACT.Copy).then_inc(ct_ready, 1)
                experts(k, par, kk, 4)
                experts(k, par, kk, 5)
                if has(kk, 1):
                    if later(kk, 1, 1):
                        act.wait_ge(x2_mm, k - 1)
                    norm(x1[:, nxt, :], rstd2, xn2[:], r2, k - 1, xn2_ready)
                experts(k, par, kk, 6)
                if has(kk, 1):
                    act.wait_ge(x2_mm, k)
                    if later(kk, 1, 2):
                        act.wait_ge(h_mm, (k - 3) * E_N + E_N)
                    nc.scalar.activation(xn2_t[:, nxt, :], ps_x2, ACT.Copy).then_inc(x2_ready, 1)
                experts(k, par, kk, 7)
                if has(kk, 1):
                    act.wait_ge(dl_ready, k)
                    nc.scalar.activation(el[:], dl[:], ACT.Exp, accum_out=esum[:]).then_inc(el_ready, 1)
                front(k, par, kk)

            act.wait_ge(w_kv, 80)
            act.wait_ge(k_mm, 1)
            nc.scalar.activation(k_t[:], ps_s[:, 0:8, :], ACT.Identity, bias=bk[:]).then_inc(k_ready, 1)
            for kk in (-2,):
                step(kk, 0, kk)
            act.wait_ge(v_mm, 1)
            act.wait_ge(vb_zero, 3)
            for half in range(2):
                rows = slice(64 * half, 64 * half + 64)
                src = ps_p[rows, :, :].rearrange("p b (j h d) -> p b j h d", h=2, d=HD)[:, :, :, half, :]
                nc.scalar.activation(vb[rows, :, :, half * HD:half * HD + HD], src, ACT.Copy).then_inc(v_ready, 1)
            act.wait_ge(w_late, 64)
            nc.scalar.activation(tg[:], gates[:], ACT.Tanh).then_inc(gate_ready, 1)
            run(step, -1, TILES + 2)(act)

        @block.vector
        def _(dve):
            halves = (slice(0, 8), slice(8, 16))

            def find(k, par, r):
                for u, heads in enumerate(halves):
                    if r == 0:
                        dve.wait_ge(s_ready, k + 1)
                    else:
                        dve.wait_ge(removed, k * 8 + 2 * r - 1 + u)
                    dve.nop(nofuse=True)
                    src = s_sb[:, par] if r == 0 else work
                    dst = v8[:, par] if r == 0 else vr[:, r % 2]
                    for h in range(heads.start, heads.stop):
                        last = nc.vector.max(dst[:, h, :], src[:, h, :])
                    last.then_inc(found, 1)

            def remove(k, par, r):
                for u, heads in enumerate(halves):
                    dve.wait_ge(found, k * 8 + 2 * r + 1 + u)
                    dve.nop(nofuse=True)
                    src = s_sb[:, par] if r == 0 else work
                    vals = v8[:, par] if r == 0 else vr[:, r % 2]
                    for h in range(heads.start, heads.stop):
                        last = nc.vector.match_replace(work[:, h, :], vals[:, h, :], src[:, h, :], NEG)
                    last.then_inc(removed, 1)

            def add_expert(k, par, kk, e):
                if not has(kk, 2):
                    return
                n = (k - 2) * E_N + e
                dve.wait_ge(y_mm, n + 1)
                if e > 0 or kk is None or kk > 2:
                    dve.wait_ge(acc_done, n)
                nc.vector.scalar_tensor_tensor(x1[:, par, :], ps_y[e % 2], route[:, par, e:e + 1], x1[:, par, :],
                                               ALU.mult, ALU.add).then_inc(acc_done, 1)

            def step(k, par, kk):
                nxt = (par + 1) % 2
                sel, att, fr = has(kk, 0), has(kk, 1), has(kk, -2)
                if sel:
                    if later(kk, 0, 2):
                        dve.wait_ge(d_ready, k - 1)
                    find(k, par, 0)
                    remove(k, par, 0)
                if fr:
                    if kk == -2:
                        dve.wait_ge(x_first, 16)
                    if kk == 0:
                        dve.wait_ge(x_rest, 16)
                    if later(kk, -2, 2):
                        dve.wait_ge(r1, k + 1)
                    nc.vector.bn_stats(stats[:, par, :], x_all[:, bass.ds(k + 2, 1), :].rearrange("p a d -> p (a d)")
                                       ).then_inc(st1_raw, 1)
                    dve.wait_ge(st1_raw, k + 3)
                    dve.nop(nofuse=True)
                    nc.vector.bn_aggr(mv[:, par, :], stats[:, par, :]).then_inc(st1, 1)
                if sel:
                    find(k, par, 1)
                    remove(k, par, 1)
                add_expert(k, par, kk, 0)
                if att:
                    dve.wait_ge(pv_mm, k)
                    den = ps_pv[:, :, 2 * HD:VW]
                    nc.vector.reciprocal(rden[:].rearrange("p (j h) -> p j h", h=2), den).then_inc(rden_ready, 1)
                    dve.wait_ge(rden_ready, k)
                    nc.vector.tensor_tensor(cn[:].rearrange("p (j h d) -> p j h d", h=2, d=HD),
                                            ps_pv[:, :, 0:2 * HD].rearrange("p j (h d) -> p j h d", h=2),
                                            rden[:].rearrange("p (j h) -> p j h", h=2).unsqueeze(3).to_broadcast([P, PAIRS, 2, HD]),
                                            ALU.mult).then_inc(cn_ready, 1)
                add_expert(k, par, kk, 1)
                if sel:
                    find(k, par, 2)
                    remove(k, par, 2)
                add_expert(k, par, kk, 2)
                if att:
                    dve.wait_ge(o_mm, k)
                    if kk == 1:
                        dve.wait_ge(gate_ready, 1)
                    if later(kk, 1, 2):
                        dve.wait_ge(stored, (k - 2) * 16)
                    nc.vector.scalar_tensor_tensor(x1[:, nxt, :], ps_o, tg[:, 0:1],
                                                   x_all[:, bass.ds(k - 1, 1), :].rearrange("p a d -> p (a d)"),
                                                   ALU.mult, ALU.add).then_inc(x1_ready, 1)
                    dve.wait_ge(x1_ready, k)
                    nc.vector.bn_stats(stats2[:], x1[:, nxt, :]).then_inc(st2_raw, 1)
                    dve.wait_ge(st2_raw, k)
                    if later(kk, 1, 1):
                        dve.wait_ge(r2, k - 1)
                    dve.nop(nofuse=True)
                    nc.vector.bn_aggr(mv2[:], stats2[:]).then_inc(st2, 1)
                add_expert(k, par, kk, 3)
                if sel:
                    find(k, par, 3)
                add_expert(k, par, kk, 4)
                add_expert(k, par, kk, 5)
                if att:
                    dve.wait_ge(l_mm, k)
                    dve.nop(nofuse=True)
                    nc.vector.max(top8[:], ps_l).then_inc(top_ready, 1)
                    dve.wait_ge(top_ready, k)
                    if later(kk, 1, 1):
                        dve.wait_ge(el_ready, k - 1)
                    nc.vector.tensor_scalar(dl[:], top8[:], top8[:, 0:1], None, ALU.subtract).then_inc(dl_ready, 1)
                    nc.vector.max_index(idx8[:], top8[:], ps_l).then_inc(idx_ready, 1)
                if sel:
                    remove(k, par, 3)
                add_expert(k, par, kk, 6)
                add_expert(k, par, kk, 7)
                if att:
                    dve.wait_ge(el_ready, k)
                    nc.vector.reciprocal(wgt[:, 0:1], esum[:]).then_inc(wgt_a, 1)
                    dve.wait_ge(idx_ready, k)
                    nc.vector.tensor_copy(idxf[:], idx8[:, 0:1]).then_inc(wgt_b, 1)
                    dve.wait_ge(wgt_a, k)
                    nc.vector.tensor_scalar(wgt[:, 1:2], wgt[:, 0:1], tg[:, 1:2], None, ALU.mult).then_inc(wgt_b, 1)
                    dve.wait_ge(wgt_b, 2 * k)
                    nc.vector.tensor_scalar(route[:, nxt, :], iota8, idxf[:], wgt[:, 1:2], ALU.is_equal, ALU.mult
                                            ).then_inc(route_ready, 1)
                    dve.wait_ge(route_ready, k)
                if sel:
                    dve.wait_ge(e_ready, k + 1)
                    dve.wait_ge(removed, k * 8 + 8)
                    if later(kk, 0, 2):
                        dve.wait_ge(p_mm, k - 1)
                    nc.vector.scalar_tensor_tensor(p_sb[:, par].rearrange("p j c -> p (j c)"),
                                                   work[:].rearrange("p h n -> p (h n)"), NEG,
                                                   e_sb[:].rearrange("p h n -> p (h n)"),
                                                   ALU.is_equal, ALU.mult).then_inc(p_ready, 1)
            dve.wait_ge(consts_in, 16)
            run(step, -2, TILES + 2)(dve)

        @block.tensor
        def _(pe):
            def hidden(k, par, kk, e):
                if not has(kk, 2):
                    return
                n = (k - 2) * E_N + e
                if kk is None or kk > 2 or e >= 2:
                    pe.wait_ge(h_ready, n - 1)
                if e == 0:
                    pe.wait_ge(x2_ready, k - 1)
                    if kk == 2:
                        pe.wait_ge(w_moe, 64)
                for c in range(FC):
                    last = nc.tensor.matmul(ps_h[e % 2][:, c, :], w1[:, e, c * P:c * P + P], xn2_t[:, par, :],
                                            start=True, stop=True)
                last.then_inc(h_mm, 1)

            def down(k, par, kk, e):
                if not has(kk, 2):
                    return
                n = (k - 2) * E_N + e
                if kk is None or kk > 2 or e >= 2:
                    pe.wait_ge(acc_done, n - 1)
                pe.wait_ge(h_ready, n + 1)
                for c in range(FC):
                    nc.tensor.matmul(ps_y[e % 2], h_t[:, e % 2, c, :], w2[:, e, c, :], start=(c == 0), stop=False)
                nc.tensor.matmul(ps_y[e % 2], ones_row[:], b2_row[:, e * D:e * D + D], start=False, stop=True
                                 ).then_inc(y_mm, 1)

            def step(k, par, kk):
                nxt = (par + 1) % 2
                att = has(kk, 1)
                if att:
                    pe.wait_ge(p_ready, k)
                    pe.wait_ge(s_ready, (k + 1) if kk is None or kk < TILES else TILES)
                    for j in range(PAIRS):
                        last = nc.tensor.transpose(ps_p[:, j, :], p_sb[:, nxt, j, :], ident)
                    last.then_inc(p_mm, 1)
                hidden(k, par, kk, 0)
                hidden(k, par, kk, 1)
                if has(kk, -1):
                    pe.wait_ge(q_ready, k + 2)
                    bb = (k + 1) // 2 if kk is not None else batch_of[0](k, par)
                    if kk == -1:
                        pe.wait_ge(v_ready, 2)
                    pe.wait_ge(kb_ready, B if kk is None or kk > 1 else bb + 1)
                    if att:
                        pe.wait_ge(pt_ready, k)
                    elif later(kk, -1, 1):
                        pe.wait_ge(s_ready, k + 1)
                    for u in range(2):
                        last = nc.tensor.matmul(ps_s[:, 8 * u:8 * u + 8, :], q_t[:, nxt, :],
                                                kb[:, bass.ds(bb, 1), 8 * u:8 * u + 8, :].rearrange("p a h n -> p (a h n)"),
                                                start=True, stop=True)
                    last.then_inc(s_mm, 1)
                if att:
                    pe.wait_ge(pt_ready, k)
                    if later(kk, 1, 1):
                        pe.wait_ge(idx_ready, k - 1)
                    bb = (k - 1) // 2 if kk is not None else batch_of[1](k, par)
                    for j in range(PAIRS):
                        last = nc.tensor.matmul(ps_pv[:, j, :], p_t[:, j, :],
                                                vb[:, bass.ds(bb, 1), j, :].rearrange("p a v -> p (a v)"), start=True, stop=True)
                    last.then_inc(pv_mm, 1)
                down(k, par, kk, 0)
                hidden(k, par, kk, 2)
                down(k, par, kk, 1)
                hidden(k, par, kk, 3)
                if att:
                    pe.wait_ge(cn_ready, k)
                    nc.tensor.transpose(ps_c, cn[:], ident).then_inc(c_mm, 1)
                down(k, par, kk, 2)
                hidden(k, par, kk, 4)
                if att:
                    pe.wait_ge(ct_ready, k)
                    if kk == 1:
                        pe.wait_ge(w_late, 64)
                        pe.wait_ge(consts_set, 2)
                    nc.tensor.matmul(ps_o, c_t[:], wo[:], start=True, stop=False)
                    nc.tensor.matmul(ps_o, ones_row[:], bo_row[:], start=False, stop=True).then_inc(o_mm, 1)
                down(k, par, kk, 3)
                hidden(k, par, kk, 5)
                down(k, par, kk, 4)
                hidden(k, par, kk, 6)
                if att:
                    pe.wait_ge(xn2_ready, k)
                    nc.tensor.transpose(ps_x2, xn2[:], ident).then_inc(x2_mm, 1)
                down(k, par, kk, 5)
                hidden(k, par, kk, 7)
                if att:
                    pe.wait_ge(x2_ready, k)
                    nc.tensor.matmul(ps_l, xn2_t[:, nxt, :], wr[:], start=True, stop=True).then_inc(l_mm, 1)
                down(k, par, kk, 6)
                down(k, par, kk, 7)
                if has(kk, -2):
                    pe.wait_ge(xn_ready, k + 3)
                    if later(kk, -2, 1):
                        pe.wait_ge(q_ready, k + 2)
                    nc.tensor.transpose(ps_xt, xn[:, par, :], ident).then_inc(xt_mm, 1)
                    pe.wait_ge(xt_ready, k + 3)
                    if kk == -2:
                        pe.wait_ge(w_q, 32)
                    nc.tensor.matmul(ps_q, wq[:], xn_t[:, par, :], start=True, stop=True).then_inc(q_mm, 1)

            pe.wait_ge(w_kv, 80)
            nc.tensor.matmul(ps_s[:, 0:8, :], wk[:], ctx_t[:, :, 0, :], start=True, stop=True).then_inc(k_mm, 1)
            pe.wait_ge(consts_set, 2)
            pe.wait_ge(k_ready, 1)
            for b in range(B):
                nc.tensor.matmul(ps_p[:, b, :], ctx_t[:, b, :, :].rearrange("p a n -> p (a n)"), wv[:], start=True, stop=False)
                last = nc.tensor.matmul(ps_p[:, b, :], ones_row[:], bv_row[:], start=False, stop=True)
            last.then_inc(v_mm, 1)
            pe.wait_ge(consts_in, 16)
            batch_of = (lambda k, par: loop_half[0] + (1 if par else 0), lambda k, par: loop_half[0] - (0 if par else 1))
            loop_half = [None]
            for k in range(-2, LOOP_FROM):
                step(k, k % 2, k)
            with pe.Fori(LOOP_FROM // 2, LOOP_TO // 2) as i:
                loop_half[0] = i
                step(i * 2, 0, None)
                step(i * 2 + 1, 1, None)
            for k in range(LOOP_TO, TILES + 2):
                step(k, k % 2, k)


def kernel(**inputs):
    import concourse.bacc as bacc
    from concourse.bass_utils import run_bass_kernel_spmd
    a = {n: np.asarray(v) for n, v in inputs.items()}
    L = "L0_xattn_"
    M = "L0_ffn_"
    const = np.zeros((P, C_W), np.float32)
    const[:, C_ID:C_ID + P] = np.eye(P, dtype=np.float32)
    const[np.arange(P), C_HM + np.arange(P) // HD] = 1.0
    const[:, C_IOTA:C_IOTA + E_N] = np.arange(E_N, dtype=np.float32)
    c = a["ctx_1024"].transpose(2, 0, 1)
    arrays = {
        "x": a["x"].reshape(TILES, P, D).transpose(1, 0, 2),
        "const": const,
        "wq": a[L + "Wq"].T, "wk": a[L + "Wk"].T, "wv": a[L + "Wv"].T, "wo": a[L + "Wo"].T,
        "bq": a[L + "bq"].reshape(P, 1), "bk": a[L + "bk"].reshape(P, 1),
        "bv": a[L + "bv"].reshape(1, D), "bo": a[L + "bo"].reshape(1, D),
        "ctx": np.stack([c, c], axis=2),
        "gates": np.broadcast_to(np.concatenate([a["g_xattn"], a["g_ffn"]])[None, :], (P, 2)),
        "wr": a[M + "w_router"],
        "w1": a[M + "w1"].transpose(1, 0, 2),
        "b1": a[M + "b1"].reshape(E_N, FC, P).transpose(2, 0, 1).reshape(P, E_N * FC),
        "w2": a[M + "w2"].reshape(E_N, FC, P, D).transpose(2, 0, 1, 3),
        "b2": a[M + "b2"].reshape(1, E_N * D),
    }
    nc = bacc.Bacc("TRN2", target_bir_lowering=False, num_devices=1)
    t, feed = {}, {}
    for n, v in arrays.items():
        v = np.ascontiguousarray(v)
        feed["in_" + n] = v
        t[n] = nc.dram_tensor("in_" + n, v.shape, F32, kind="ExternalInput").ap()
    out = nc.dram_tensor("out", (TILES, P, D), F32, kind="ExternalOutput").ap()
    t["out"] = out.rearrange("t p d -> p t d")
    build(nc, t)
    r = run_bass_kernel_spmd(nc, [feed], core_ids=[0])
    return r.results[0]["out"].reshape(B, S, D)
```

```python
import concourse.bass as bass
import numpy as np
from concourse import mybir
from contextlib import ExitStack

F32 = mybir.dt.float32
BF16 = mybir.dt.bfloat16
I32 = mybir.dt.int32
U32 = mybir.dt.uint32
ALU = mybir.AluOpType
ACT = mybir.ActivationFunctionType
AX = mybir.AxisListType

P = 128
B, S, D = 8, 256, 128
N = 64
HEADS = 16
HD = D // HEADS
TOPK = 32
E_N = 8
F = 512
FC = F // P
TILES = B * S // P
PAIRS = HEADS // 2
VW = 2 * HD + 2
SCALE = float(HD) ** -0.5
NEG = -3.0e38
DROP = -float(2 ** 100)
HN = N // 2
HALF = TOPK // 2
DROPPED = P * HEADS * (N - TOPK)
REMOVED = P * 2 * HEADS * 8
EPS = 1e-5

CHUNKS = 2
CT = TILES // CHUNKS
UNITS = CT + E_N - 1
RINGS = (4, 6)
PLACES = (range(0, 4), range(4, 10))
TURN_FIRST = 1
WW = 2 * F + FC + D

C_ID, C_HM, C_IOTA = 0, 128, 144
C_EDGE = C_IOTA + E_N
C_UPTO = C_EDGE + CT
C_UNIT = C_UPTO + E_N * E_N
C_BEFORE = C_UNIT + UNITS
C_W = C_BEFORE + P

LOOPS = ((4, 8), (10, 14))
PLANS, PLACED = 10, 6
FIRST_UNITS = 10
TILE_UNITS = 2 * (TILES - FIRST_UNITS)


def build(nc, t):
    ctx = ExitStack()
    with ctx:
        def sb(name, shape, dt=F32):
            return ctx.enter_context(nc.sbuf_tensor(name, shape, dt))

        def ps(name, shape):
            return ctx.enter_context(nc.psum_tensor(name, shape, F32))

        def sem(name):
            return ctx.enter_context(nc.semaphore(name))

        x_all = sb("x_all", [P, TILES, D])
        const = sb("const", [P, C_W])
        ident = const[:, C_ID:C_ID + P]
        head_mask = const[:, C_HM:C_HM + HEADS]
        iota8 = const[:, C_IOTA:C_IOTA + E_N]
        edges = const[:, C_EDGE:C_EDGE + CT]
        upto_mask = const[:, C_UPTO:C_UPTO + E_N * E_N]
        unit_no = const[:, C_UNIT:C_UNIT + UNITS]
        ones_row = sb("ones_row", [1, P])
        ones_col = sb("ones_col", [P, 1])
        removed_weight = sb("removed_weight", [P, 1])
        less_dropped = sb("less_dropped", [1, 1])
        half_neg = sb("half_neg", [P, 1])
        lowest = sb("lowest", [P, 1])
        wq = sb("wq", [P, D])
        wk = sb("wk", [P, D])
        wv = sb("wv", [P, D])
        wo = sb("wo", [P, D])
        wr = sb("wr", [P, E_N])
        ctx_t = sb("ctx_t", [P, B, N])
        ctx_twice = sb("ctx_twice", [P, B, 2, N])
        bq = sb("bq", [P, 1])
        bk = sb("bk", [P, 1])
        bv_row = sb("bv_row", [1, D])
        bo_row = sb("bo_row", [1, D])
        gates = sb("gates", [P, 2])
        tg = sb("tg", [P, 2])
        k_t = sb("k_t", [P, B, N])
        kb = sb("kb", [P, B, HEADS, N])
        vb = sb("vb", [P, B, PAIRS, VW])
        stats = sb("stats", [P, 2, 6])
        mv = sb("mv", [P, 2, 2])
        rstd = sb("rstd", [P, 2, 3])
        xn = sb("xn", [P, 2, D])
        xn_t = sb("xn_t", [P, 2, P])
        q_t = sb("q_t", [P, 2, P])
        s_sb = sb("s_sb", [P, 2, HEADS, N])
        hi = sb("hi", [P, HEADS, HN])
        pairs = sb("pairs", [P, 2, 2 * HEADS, HN])
        rest = sb("rest", [P, 2 * HEADS, HN])
        ranks = sb("ranks", [P, 2 * HEADS, HALF])
        cross = sb("cross", [P, HEADS, HALF])
        limit = sb("limit", [P, HEADS])
        row_max = sb("row_max", [P, 2, HEADS])
        z_sb = sb("z_sb", [P, 2, PAIRS, P])
        drop = sb("drop", [P, 2, HEADS, N], BF16)
        top_mark = sb("top_mark", [P, 2 * HEADS, HN], BF16)
        count = sb("count", [P, 3])
        count_sq = sb("count_sq", [1, 2])
        count_off = sb("count_off", [1, 1])
        work = sb("work", [P, HEADS, N])
        work8 = sb("work8", [P, HEADS, 8])
        drop_id = sb("drop_id", [P, P], BF16)
        p_t = sb("p_t", [P, PAIRS, P])
        rden = sb("rden", [P, HEADS])
        cn = sb("cn", [P, D])
        c_t = sb("c_t", [P, P])
        x1_all = sb("x1_all", [P, TILES, D])
        stats2 = sb("stats2", [P, 6])
        mv2 = sb("mv2", [P, 2])
        rstd2 = sb("rstd2", [P, 3])
        xn2 = sb("xn2", [P, 2, D])
        xn2_all = sb("xn2_all", [P, TILES, D])
        xn2_t = sb("xn2_t", [P, P])
        top8 = sb("top8", [P, 8])
        idx8 = sb("idx8", [P, 8], U32)
        idxf = sb("idxf", [P, 1])
        dl = sb("dl", [P, 8])
        el = sb("el", [P, 8])
        esum = sb("esum", [P, 1])
        share = sb("share", [P, 1])
        share_all = sb("share_all", [P, TILES])
        chosen = sb("chosen", [P, TILES, E_N], BF16)
        before = sb("before", [P, P], BF16)
        ones_bf = sb("ones_bf", [P, P], BF16)
        full = sb("full", [P, E_N, CT])
        n_units = sb("n_units", [P, E_N])
        upto = sb("upto", [P, E_N, E_N])
        last_unit = sb("last_unit", [P, E_N])
        first_unit = sb("first_unit", [P, E_N])
        place = sb("place", [P, CT, E_N])
        place_own = sb("place_own", [P, CT, E_N])
        slot_f = sb("slot_f", [P, CT])
        slot = sb("slot", [P, CHUNKS, CT], U32)
        past = sb("past", [1, UNITS, E_N])
        expert_f = sb("expert_f", [1, UNITS])
        expert = sb("expert", [1, CHUNKS, UNITS], I32)
        zeros = sb("zeros", [P, D])
        w_ring = sb("w_ring", [P, sum(RINGS), WW])
        xs_ring = sb("xs_ring", [P, sum(RINGS), D])
        xs_t = sb("xs_t", [P, 2, P])
        h_t = sb("h_t", [P, 2, FC, P])
        y_all = sb("y_all", [P, 2 * UNITS, D])
        y_back = x_all[:].rearrange("p (c t) d -> p c t d", c=CHUNKS)

        ps_s = ps("ps_s", [P, HEADS, N])
        ps_p = ps("ps_p", [P, PAIRS, P])
        ps_h = [ps("ps_h", [P, FC, P]), ps_s[:, 0:HEADS // 2, :].rearrange("p (c q) n -> p c (q n)", c=FC)]
        ps_y = [ps("ps_y", [P, 512])[:, 0:D], ps_p[:, 0, :]]
        ps_front = ps("ps_front", [P, 512])
        ps_xt, ps_q, ps_xs = ps_front[:, 0:128], ps_front[:, 128:256], ps_front[:, 256:384]
        ps_rank = ps_front[:, 384:384 + CT * E_N].rearrange("p (t e) -> p t e", e=E_N)
        ps_total = ps_front[:, 384 + CT * E_N:384 + (CT + 1) * E_N]
        ps_att = ps("ps_att", [P, 512])
        ps_pv = ps_att[:, 0:PAIRS * VW].rearrange("p (j v) -> p j v", v=VW)
        ps_c = ps_x2 = ps_att[:, 144:272]
        ps_o = ps_att[:, 272:400]
        ps_l = ps_att[:, 400:408]
        ps_count = ps_att[0:1, 408:410]

        x_first, x_rest = sem("x_first"), sem("x_rest")
        w_q, w_kv, w_v, w_late, w_moe, consts_in = sem("w_q"), sem("w_kv"), sem("w_v"), sem("w_late"), sem("w_moe"), sem("consts_in")
        consts_set, gate_ready = sem("consts_set"), sem("gate_ready")
        k_mm, k_ready, kb_zero, kb_ready = sem("k_mm"), sem("k_ready"), sem("kb_zero"), sem("kb_ready")
        v_mm, vb_zero, v_ready = sem("v_mm"), sem("vb_zero"), sem("v_ready")
        st1_raw, st1, var1, rsq1, r1 = sem("st1_raw"), sem("st1"), sem("var1"), sem("rsq1"), sem("r1")
        xn_ready, xt_mm, xt_ready, q_mm, q_ready = sem("xn_ready"), sem("xt_mm"), sem("xt_ready"), sem("q_mm"), sem("q_ready")
        s_mm, s_ready = sem("s_mm"), sem("s_ready")
        paired, max_ready, negated = sem("paired"), sem("max_ready"), sem("negated")
        found, marked, penalised, removed = sem("found"), sem("marked"), sem("penalised"), sem("removed")
        crossed, limit_ready, drop_ready, z_ready = sem("crossed"), sem("limit_ready"), sem("drop_ready"), sem("z_ready")
        count_mm, count_read, drop_ok = sem("count_mm"), sem("count_read"), sem("drop_ok")
        drop_id_set, p_mm, pt_ready = sem("drop_id_set"), sem("p_mm"), sem("pt_ready")
        pv_mm, rden_ready, cn_ready, c_mm, ct_ready, o_mm = sem("pv_mm"), sem("rden_ready"), sem("cn_ready"), sem("c_mm"), sem("ct_ready"), sem("o_mm")
        x1_ready = sem("x1_ready")
        st2_raw, st2, var2, rsq2, r2 = sem("st2_raw"), sem("st2"), sem("var2"), sem("rsq2"), sem("r2")
        xn2_kept = sem("xn2_kept")
        xn2_ready, x2_mm, x2_ready, l_mm = sem("xn2_ready"), sem("x2_mm"), sem("x2_ready"), sem("l_mm")
        top_ready, dl_ready, el_ready, idx_ready = sem("top_ready"), sem("dl_ready"), sem("el_ready"), sem("idx_ready")
        share_a, idxf_ready, share_ready, chosen_ready = sem("share_a"), sem("idxf_ready"), sem("share_ready"), sem("chosen_ready")
        rank_mm, plan = sem("rank_mm"), sem("plan")
        slot_ready, expert_ready, scattered, cleared = sem("slot_ready"), sem("expert_ready"), sem("scattered"), sem("cleared")
        zeros_set, before_set = sem("zeros_set"), sem("before_set")
        w_in = [sem(f"w_in{i}") for i in range(sum(RINGS))]
        xs_in = [sem(f"xs_in{i}") for i in range(sum(RINGS))]
        xs_mm, xs_ready, h_mm, h_ready, y_mm, y_ready = (sem("xs_mm"), sem("xs_ready"), sem("h_mm"), sem("h_ready"),
                                                        sem("y_mm"), sem("y_ready"))
        out_ready, stored = sem("out_ready"), sem("stored")
        y_out = [sem(f"y_out{ch}") for ch in range(CHUNKS)]
        y_in = [[sem(f"y_in{ch}_{tt}") for tt in range(CT)] for ch in range(CHUNKS)]

        block = ctx.enter_context(nc.Block())

        class Unit:
            def __init__(self, chunk, turn, r, even=0):
                self.chunk, self.slot, self.uses = chunk, PLACES[chunk][r], turn + 1
                self.j = turn * RINGS[chunk] + r
                self.n = self.j + chunk * UNITS
                self.par = even if type(turn) is not int else self.n % 2
                beside_tiles = chunk == 0 and (type(turn) is not int or self.n < TILE_UNITS)
                self.bank, self.back = (0, 1) if beside_tiles else (self.par, 2)

        def unit(chunk, j):
            return Unit(chunk, j // RINGS[chunk], j % RINGS[chunk])

        def run(step_of, first, last):
            def go(eng):
                def peeled(k):
                    j = 2 * (k - FIRST_UNITS)
                    js = range(j, j + 2) if FIRST_UNITS <= k < TILES else ()
                    step_of(k, k % 2, k, k // 2, [unit(0, j) for j in js])

                k = first
                for a, b in LOOPS:
                    for k in range(k, min(a, last)):
                        peeled(k)
                    with eng.Fori(a // 2, b // 2) as i:
                        for par in range(2):
                            cs = range(2 * (par - FIRST_UNITS), 2 * (par - FIRST_UNITS) + 2) if a >= FIRST_UNITS else ()
                            step_of(i * 2 + par, par, None, i,
                                    [Unit(0, i + c // RINGS[0], c % RINGS[0], c % 2) for c in cs])
                    k = b
                for k in range(k, last):
                    peeled(k)
            return go

        def units_after(eng, rows, hidden, out):
            first = [unit(0, j) for j in range(TILE_UNITS, UNITS)] + [unit(1, j) for j in range(TURN_FIRST)]
            last = [unit(1, j) for j in range(TURN_FIRST + 2 * RINGS[1], UNITS)]

            def three(u):
                rows(u[2])
                hidden(u[1])
                out(u[0])
            rows(first[0])
            rows(first[1])
            hidden(first[0])
            ahead = [unit(1, TURN_FIRST + i) for i in range(2)]
            for i in range(len(first)):
                three((first + ahead)[i:i + 3])
            with eng.Fori(0, 2) as i:
                for r in range(TURN_FIRST, TURN_FIRST + RINGS[1]):
                    three([Unit(1, i + (r + d) // RINGS[1], (r + d) % RINGS[1], (r + d + UNITS) % 2) for d in range(3)])
            for i in range(len(last) - 2):
                three(last[i:i + 3])
            hidden(last[-1])
            out(last[-2])
            out(last[-1])

        def has(k, lag):
            return k is None or 0 <= k - lag < TILES

        def later(k, lag, n):
            return k is None or k - lag >= n


        @block.sync
        def _(sp):
            sp.dma_start(x_all[:, 0:2, :], t["x"][:, 0:2, :]).then_inc(x_first, 16)
            sp.dma_start(const[:], t["const"]).then_inc(consts_in, 16)
            sp.dma_start(wq[:], t["wq"]).then_inc(w_q, 16)
            sp.dma_start(bq[:], t["bq"]).then_inc(w_q, 16)
            sp.wait_ge(k_ready, 1)
            sp.dma_start(x_all[:, 2:TILES, :], t["x"][:, 2:TILES, :]).then_inc(x_rest, 16)
            sp.wait_ge(zeros_set, 1)
            sp.wait_ge(s_ready, 1)
            for ch in range(CHUNKS):
                sp.dma_start(t["xs"][ch].rearrange("(j p) d -> p j d", p=P),
                             zeros[:].unsqueeze(1).to_broadcast([P, UNITS, D])).then_inc(cleared, 16)

            def unit_expert(u):
                return sp.value_load(expert[0:1, u.chunk, bass.ds(u.j, 1)], min_val=0, max_val=E_N - 1)

            def load_weights(u, e):
                sp.dma_start(w_ring[:, u.slot, :], t["w"][bass.ds(e, 1), :, :].rearrange("a p n -> (a p) n")
                             ).then_inc(w_in[u.slot], 16)

            def load_rows(u):
                sp.dma_start(xs_ring[:, u.slot, :], t["xs"][u.chunk][bass.ds(u.j * P, P), :]).then_inc(xs_in[u.slot], 16)

            def first_loads(ch):
                sp.wait_ge(expert_ready, ch + 1)
                for r in range(2):
                    load_weights(unit(ch, r), unit_expert(unit(ch, r)))
                sp.wait_ge(scattered, 16 * CT * (ch + 1))
                for r in range(RINGS[ch]):
                    load_rows(unit(ch, r))
                    if r >= 2:
                        load_weights(unit(ch, r), unit_expert(unit(ch, r)))

            def store_then_load(u, ahead):
                if ahead:
                    e = unit_expert(ahead)
                sp.wait_ge(y_ready, u.n + 3)
                sp.dma_start(t["ys"][u.chunk][bass.ds(u.j * P, P), :],
                             y_all[:, bass.ds(u.n, 1), :].rearrange("p a d -> p (a d)")).then_inc(y_out[u.chunk], 16)
                if ahead:
                    load_weights(ahead, e)
                    load_rows(ahead)

            def stores_and_loads(ch):
                ring = RINGS[ch]
                turns = (UNITS - ring) // ring
                with sp.Fori(0, turns) as i:
                    for r in range(ring):
                        store_then_load(Unit(ch, i, r), Unit(ch, i + 1, r))
                for j in range(turns * ring, UNITS):
                    if ch == 0 and j == TILE_UNITS:
                        first_loads(1)
                    store_then_load(unit(ch, j), unit(ch, j + ring) if j + ring < UNITS else None)

            first_loads(0)
            stores_and_loads(0)
            stores_and_loads(1)
            for ch in range(CHUNKS):
                for tt in range(0, CT, 2):
                    sp.wait_ge(out_ready, ch * CT + tt + 2)
                    sp.dma_start(t["out"][:, ch * CT + tt:ch * CT + tt + 2, :], y_back[:, ch, tt:tt + 2, :]).then_inc(stored, 16)
            sp.wait_ge(stored, 16 * TILES // 2)

        @block.gpsimd
        def _(pool):
            nc.gpsimd.memset(zeros[:], 0.0).then_inc(zeros_set, 1)
            nc.gpsimd.memset(ones_row[:], 1.0).then_inc(consts_set, 1)
            nc.gpsimd.memset(half_neg[:], -0.5).then_inc(consts_set, 1)
            nc.gpsimd.memset(ones_col[:], 1.0).then_inc(consts_set, 1)
            nc.gpsimd.memset(ones_bf[:], 1.0).then_inc(consts_set, 1)
            nc.gpsimd.memset(lowest[:], NEG).then_inc(consts_set, 1)
            nc.gpsimd.memset(removed_weight[:], DROPPED / REMOVED).then_inc(consts_set, 1)
            nc.gpsimd.memset(less_dropped[:], -float(DROPPED)).then_inc(consts_set, 1)
            nc.gpsimd.memset(vb[:], 0.0).then_inc(vb_zero, 1)
            pool.wait_ge(vb_zero, 1)
            nc.gpsimd.memset(vb[0:64, :, :, 2 * HD:2 * HD + 1], 1.0).then_inc(vb_zero, 1)
            nc.gpsimd.memset(vb[64:128, :, :, 2 * HD + 1:VW], 1.0).then_inc(vb_zero, 1)
            pool.wait_ge(consts_in, 16)
            pool.wait_ge(consts_set, 7)
            pool.wait_ge(vb_zero, 3)

            def rsqrt(st_sem, var_sem, rsq_sem, r_sem, mv_, r_, n):
                pool.wait_ge(st_sem, n + 1)
                pool.nop(nofuse=True)
                nc.gpsimd.tensor_scalar(r_[:, 2:3], mv_[:, 1:2], EPS, None, ALU.add).then_inc(var_sem, 1)
                pool.wait_ge(var_sem, n + 1)
                nc.gpsimd.tensor_tensor(r_[:, 0:1], r_[:, 2:3], half_neg[:], ALU.pow).then_inc(rsq_sem, 1)
                pool.wait_ge(rsq_sem, n + 1)
                pool.nop(nofuse=True)
                nc.gpsimd.tensor_scalar(r_[:, 1:2], mv_[:, 0:1], r_[:, 0:1], -1.0, ALU.mult, ALU.mult).then_inc(r_sem, 1)

            def spread_keys(b):
                nc.gpsimd.tensor_tensor(kb[:, b, :, :], k_t[:, b, :].unsqueeze(1).to_broadcast([P, HEADS, N]),
                                        head_mask.unsqueeze(2).to_broadcast([P, HEADS, N]),
                                        ALU.mult).then_inc(kb_ready, 1)

            def scatter(ch, tiles):
                pool.wait_ge(cleared, 16 * CHUNKS)
                pool.wait_ge(slot_ready, ch + 1)
                pool.wait_ge(xn2_kept, CT * (ch + 1))
                for tt in tiles:
                    nc.gpsimd.indirect_dma_start(
                        t["xs"][ch], bass.IndirectOffsetOnAxis(slot[:, ch, tt:tt + 1], 0),
                        xn2_all[:, ch * CT + tt, :], None).then_inc(scattered, 16)

            def gather(ch):
                pool.wait_ge(y_out[ch], 16 * UNITS)
                for tt in range(CT):
                    nc.gpsimd.indirect_dma_start(
                        y_back[:, ch, tt, :], None, t["ys"][ch],
                        bass.IndirectOffsetOnAxis(slot[:, ch, tt:tt + 1], 0)).then_inc(y_in[ch][tt], 16)

            def take_out(k, par, side):
                rows = slice(side * HEADS, side * HEADS + HEADS)
                pool.wait_ge(marked, 2 * k + 1 + side)
                pool.nop(nofuse=True)
                nc.gpsimd.tensor_tensor(rest[:, rows, :], top_mark[:, rows, :], lowest[:].unsqueeze(2).to_broadcast([P, HEADS, HN]),
                                        ALU.mult).then_inc(penalised, 1)
                pool.wait_ge(penalised, 2 * k + 1 + side)
                nc.gpsimd.tensor_tensor(rest[:, rows, :], rest[:, rows, :], pairs[:, par, rows, :], ALU.add).then_inc(removed, 1)

            def step(k, par, kk, half, units):
                if has(kk, 0):
                    take_out(k, par, 0)
                    take_out(k, par, 1)
                if has(kk, 2):
                    pool.wait_ge(xn2_ready, k - 1)
                    nc.gpsimd.tensor_copy(xn2_all[:, bass.ds(k - 2, 1), :].rearrange("p a d -> p (a d)"), xn2[:, par, :]
                                          ).then_inc(xn2_kept, 1)
                if has(kk, -2):
                    rsqrt(st1, var1, rsq1, r1, mv[:, par, :], rstd[:, par, :], k + 2)
                if kk == CT + 1:
                    scatter(0, range(CT // 2))
                if kk is not None:
                    if kk == -2:
                        pool.wait_ge(k_ready, 1)
                    for b in range(2 * kk + 3, min(2 * kk + 5, B)) if kk > -2 else (0,):
                        spread_keys(b)
                if has(kk, 0):
                    pool.wait_ge(max_ready, k + 1)
                    if later(kk, 0, 2):
                        pool.wait_ge(p_mm, k - 1)
                    nc.gpsimd.tensor_tensor(z_sb[:, par].rearrange("p j (h n) -> p (j h) n", h=2), s_sb[:, par],
                                            row_max[:, par].unsqueeze(2).to_broadcast([P, HEADS, N]),
                                            ALU.subtract).then_inc(z_ready, 1)
                if has(kk, 1):
                    rsqrt(st2, var2, rsq2, r2, mv2[:], rstd2[:], k - 1)
                if kk == CT + 1:
                    scatter(0, range(CT // 2, CT))
            run(step, -2, TILES + 2)(pool)
            scatter(1, range(CT))
            gather(0)
            gather(1)

        @block.scalar
        def _(act):
            act.dma_start(wk[:], t["wk"]).then_inc(w_kv, 16)
            act.dma_start(ctx_t[:], t["ctx"]).then_inc(w_kv, 16)
            act.dma_start(bk[:], t["bk"]).then_inc(w_kv, 16)
            act.dma_start(ctx_twice[:], t["ctx"].unsqueeze(2).to_broadcast([P, B, 2, N])).then_inc(w_v, 16)
            act.dma_start(wv[:], t["wv"]).then_inc(w_v, 16)
            act.dma_start(bv_row[:], t["bv"]).then_inc(w_v, 16)
            act.dma_start(gates[:], t["gates"]).then_inc(w_late, 16)
            act.dma_start(wo[:], t["wo"]).then_inc(w_late, 16)
            act.dma_start(bo_row[:], t["bo"]).then_inc(w_late, 16)
            act.dma_start(wr[:], t["wr"]).then_inc(w_late, 16)
            for free_two in (xs_ready, h_ready, y_ready):
                act.sem_inc(free_two, 2)

            def norm(xin, r_, out, r_sem, n, out_sem):
                act.wait_ge(r_sem, n + 1)
                nc.scalar.activation(out, xin, ACT.Identity, scale=r_[:, 0:1], bias=r_[:, 1:2]).then_inc(out_sem, 1)

            def unit_rows(u):
                act.wait_ge(xs_mm, u.n + 1)
                act.wait_ge(h_mm, u.n + 1)
                nc.scalar.activation(xs_t[:, u.par, :], ps_xs, ACT.Copy).then_inc(xs_ready, 1)

            def unit_hidden(u):
                act.wait_ge(h_mm, u.n + 3)
                act.wait_ge(y_mm, u.n + 1)
                for c in range(FC):
                    last = nc.scalar.activation(h_t[:, u.par, c, :], ps_h[u.bank][:, c, :], ACT.Relu,
                                                bias=w_ring[:, u.slot, 2 * F + c:2 * F + c + 1])
                last.then_inc(h_ready, 1)

            def unit_out(u):
                act.wait_ge(y_mm, u.n + 3)
                nc.scalar.activation(y_all[:, bass.ds(u.n, 1), :].rearrange("p a d -> p (a d)"), ps_y[u.bank], ACT.Copy
                                     ).then_inc(y_ready, 1)

            def step(k, par, kk, half, units):
                nxt = (par + 1) % 2
                sel, att, rou = has(kk, 0), has(kk, 1), has(kk, 2)
                u = units or [None, None]
                if u[0]:
                    unit_rows(u[0])
                if rou:
                    if later(kk, 2, 1):
                        act.wait_ge(xn2_kept, k - 2)
                    norm(x1_all[:, bass.ds(k - 2, 1), :], rstd2, xn2[:, par, :], r2, k - 2, xn2_ready)
                if rou:
                    act.wait_ge(x2_mm, k - 1)
                    nc.scalar.activation(xn2_t[:], ps_x2, ACT.Copy).then_inc(x2_ready, 1)
                if has(kk, -1):
                    act.wait_ge(s_mm, k + 2)
                    if later(kk, -1, 2):
                        act.wait_ge(z_ready, k)
                        act.wait_ge(drop_ok, k)
                    nc.scalar.activation(s_sb[:, nxt], ps_s[:], ACT.Copy).then_inc(s_ready, 1)
                if att:
                    act.wait_ge(p_mm, k)
                    if later(kk, 1, 1):
                        act.wait_ge(pv_mm, k - 1)
                    nc.scalar.activation(p_t[:], ps_p[:], ACT.Exp, scale=SCALE).then_inc(pt_ready, 1)
                if u[0]:
                    unit_hidden(u[0])
                if rou:
                    act.wait_ge(dl_ready, k - 1)
                    nc.scalar.activation(el[:], dl[:], ACT.Exp, accum_out=esum[:]).then_inc(el_ready, 1)
                if u[1]:
                    unit_rows(u[1])
                if u[0]:
                    unit_out(u[0])
                if u[1]:
                    unit_hidden(u[1])
                if att:
                    act.wait_ge(c_mm, k)
                    if later(kk, 1, 1):
                        act.wait_ge(o_mm, k - 1)
                    nc.scalar.activation(c_t[:], ps_c, ACT.Copy).then_inc(ct_ready, 1)
                if has(kk, -2):
                    norm(x_all[:, bass.ds(k + 2, 1), :], rstd[:, par, :], xn[:, par, :], r1, k + 2, xn_ready)
                if kk == -2:
                    act.wait_ge(w_kv, 48)
                    act.wait_ge(k_mm, 1)
                    nc.scalar.activation(k_t[:], ps_s[:, 0:8, :], ACT.Identity, bias=bk[:]).then_inc(k_ready, 1)
                if has(kk, -2):
                    act.wait_ge(xt_mm, k + 3)
                    nc.scalar.activation(xn_t[:, par, :], ps_xt, ACT.Copy).then_inc(xt_ready, 1)
                if has(kk, -2):
                    if kk == -2:
                        act.wait_ge(w_q, 32)
                    act.wait_ge(q_mm, k + 3)
                    nc.scalar.activation(q_t[:, par, :], ps_q, ACT.Identity, bias=bq[:]).then_inc(q_ready, 1)
                if has(kk, -1):
                    act.wait_ge(paired, 2 * k + 3)
                    if later(kk, -1, 2):
                        act.wait_ge(removed, 2 * k)
                    nc.scalar.activation(pairs[:, nxt, HEADS:2 * HEADS, :], hi[:], ACT.Copy, scale=-1.0).then_inc(negated, 1)
                if u[1]:
                    unit_out(u[1])
                if sel:
                    act.wait_ge(count_mm, k + 1)
                    if later(kk, 0, 1):
                        act.wait_ge(drop_ok, k)
                    nc.scalar.activation(count_sq[:], ps_count, ACT.Square, bias=less_dropped[:], accum_out=count_off[:]
                                         ).then_inc(count_read, 1)
                if kk == -1:
                    act.wait_ge(v_mm, 1)
                    act.wait_ge(vb_zero, 3)
                    for hh in range(2):
                        rows = slice(64 * hh, 64 * hh + 64)
                        src = ps_p[rows, :, :].rearrange("p b (j h d) -> p b j h d", h=2, d=HD)[:, :, :, hh, :]
                        nc.scalar.activation(vb[rows, :, :, hh * HD:hh * HD + HD], src, ACT.Copy).then_inc(v_ready, 1)
                    act.wait_ge(w_late, 64)
                    nc.scalar.activation(tg[:], gates[:], ACT.Tanh).then_inc(gate_ready, 1)

            run(step, -2, TILES + 2)(act)

            units_after(act, unit_rows, unit_hidden, unit_out)

        @block.vector
        def _(dve):
            def find(k, par, r, side):
                src = rest[:] if r else pairs[:, par]
                for g in range(side * HEADS, side * HEADS + HEADS):
                    last = nc.vector.max(ranks[:, g, 8 * r:8 * r + 8], src[:, g, :])
                last.then_inc(found, 1)

            def mark(k, par, side):
                rows = slice(side * HEADS, side * HEADS + HEADS)
                dve.wait_ge(found, 4 * k + 1 + side)
                if side == 0 and later(k if type(k) is int else None, 0, 1):
                    dve.wait_ge(count_mm, k)
                nc.vector.scalar_tensor_tensor(top_mark[:, rows, :], pairs[:, par, rows, :], 0.0,
                                               ranks[:, rows, 7:8].to_broadcast([P, HEADS, HN]),
                                               ALU.add, ALU.is_ge, accum_out=count[:, side:side + 1]).then_inc(marked, 1)

            def drop_exactly(par):
                dve.drain()
                nc.vector.tensor_copy(work[:], s_sb[:, par])
                with dve.Fori(0, TOPK // 8):
                    dve.drain()
                    for h in range(HEADS):
                        nc.vector.max(work8[:, h, :], work[:, h, :])
                    dve.drain()
                    for h in range(HEADS):
                        nc.vector.match_replace(work[:, h, :], work8[:, h, :], work[:, h, :], NEG)
                dve.drain()
                nc.vector.tensor_scalar(drop[:, par], work[:], NEG, None, ALU.is_gt)
                dve.drain()

            def check_ties(k, par, kk):
                if not has(kk, 1):
                    return
                nxt = (par + 1) % 2
                dve.wait_ge(count_read, k)
                dve.nop(nofuse=True)
                dve.reg_load(ties, count_off[:].bitcast(I32))
                with dve.If_ne(ties, 0):
                    drop_exactly(nxt)
                dve.sem_inc(drop_ok, 1)

            def dispatch(ch):
                p0 = PLANS * ch + 1
                dve.wait_ge(rank_mm, ch + 1)
                nc.vector.tensor_tensor(full[:], ps_total.unsqueeze(2).to_broadcast([P, E_N, CT]),
                                        edges.unsqueeze(1).to_broadcast([P, E_N, CT]), ALU.is_gt).then_inc(plan, 1)
                dve.wait_ge(plan, p0)
                nc.vector.tensor_reduce(n_units[:], full[:], AX.X, ALU.add).then_inc(plan, 1)
                dve.wait_ge(plan, p0 + 1)
                nc.vector.tensor_tensor(upto[:], n_units[:].unsqueeze(1).to_broadcast([P, E_N, E_N]),
                                        upto_mask.rearrange("p (a b) -> p a b", b=E_N), ALU.mult).then_inc(plan, 1)
                dve.wait_ge(plan, p0 + 2)
                nc.vector.tensor_reduce(last_unit[:], upto[:], AX.X, ALU.add).then_inc(plan, 1)
                dve.wait_ge(plan, p0 + 3)
                nc.vector.tensor_tensor(first_unit[:], last_unit[:], n_units[:], ALU.subtract).then_inc(plan, 1)
                dve.wait_ge(plan, p0 + 4)
                nc.vector.scalar_tensor_tensor(place[:], first_unit[:].unsqueeze(1).to_broadcast([P, CT, E_N]), float(P),
                                               ps_rank, ALU.mult, ALU.add).then_inc(plan, 1)
                dve.wait_ge(plan, PLANS * ch + PLACED)
                nc.vector.tensor_tensor(place_own[:], place[:], chosen[:, ch * CT:ch * CT + CT, :], ALU.mult).then_inc(plan, 1)
                dve.wait_ge(plan, p0 + 6)
                nc.vector.tensor_reduce(slot_f[:], place_own[:], AX.X, ALU.add).then_inc(plan, 1)
                nc.vector.tensor_tensor(past[:], last_unit[0:1, :].unsqueeze(1).to_broadcast([1, UNITS, E_N]),
                                        unit_no[0:1, :].unsqueeze(2).to_broadcast([1, UNITS, E_N]), ALU.is_le).then_inc(plan, 1)
                dve.wait_ge(plan, p0 + 7)
                nc.vector.tensor_copy(slot[:, ch, :], slot_f[:]).then_inc(slot_ready, 1)
                dve.wait_ge(plan, p0 + 8)
                nc.vector.tensor_reduce(expert_f[:], past[:], AX.X, ALU.add).then_inc(plan, 1)
                dve.wait_ge(plan, p0 + 9)
                nc.vector.tensor_scalar(expert[:, ch, :], expert_f[:], float(E_N - 1), None, ALU.min).then_inc(expert_ready, 1)

            def combine(ch):
                for tt in range(CT):
                    tile = ch * CT + tt
                    dve.wait_ge(y_in[ch][tt], 16)
                    nc.vector.scalar_tensor_tensor(y_back[:, ch, tt, :], y_back[:, ch, tt, :], share_all[:, tile:tile + 1],
                                                   x1_all[:, tile, :], ALU.mult, ALU.add).then_inc(out_ready, 1)

            def step(k, par, kk, half, units):
                nxt = (par + 1) % 2
                sel, att, rou, fr, nx = has(kk, 0), has(kk, 1), has(kk, 2), has(kk, -2), has(kk, -1)
                if sel:
                    dve.wait_ge(paired, 2 * k + 2)
                    dve.nop(nofuse=True)
                    find(k, par, 0, 0)
                check_ties(k, par, kk)
                if sel:
                    mark(k, par, 0)
                    dve.wait_ge(negated, k + 1)
                    dve.nop(nofuse=True)
                    find(k, par, 0, 1)
                if rou:
                    dve.wait_ge(l_mm, k - 1)
                    dve.nop(nofuse=True)
                    nc.vector.max(top8[:], ps_l).then_inc(top_ready, 1)
                if sel:
                    mark(k, par, 1)
                if rou:
                    dve.wait_ge(top_ready, k - 1)
                    nc.vector.tensor_scalar(dl[:], top8[:], top8[:, 0:1], None, ALU.subtract).then_inc(dl_ready, 1)
                    nc.vector.max_index(idx8[:], top8[:], ps_l).then_inc(idx_ready, 1)
                if fr:
                    if kk == -2:
                        dve.wait_ge(x_first, 16)
                    if kk == 0:
                        dve.wait_ge(x_rest, 16)
                    if later(kk, -2, 2):
                        dve.wait_ge(r1, k + 1)
                    nc.vector.bn_stats(stats[:, par, :], x_all[:, bass.ds(k + 2, 1), :].rearrange("p a d -> p (a d)")
                                       ).then_inc(st1_raw, 1)
                if rou:
                    dve.wait_ge(idx_ready, k - 1)
                    nc.vector.tensor_copy(idxf[:], idx8[:, 0:1]).then_inc(idxf_ready, 1)
                if fr:
                    dve.wait_ge(st1_raw, k + 3)
                    dve.nop(nofuse=True)
                    nc.vector.bn_aggr(mv[:, par, :], stats[:, par, :]).then_inc(st1, 1)
                if rou:
                    dve.wait_ge(idxf_ready, k - 1)
                    nc.vector.tensor_scalar(chosen[:, bass.ds(k - 2, 1), :].rearrange("p a e -> p (a e)"), iota8, idxf[:],
                                            None, ALU.is_equal).then_inc(chosen_ready, 1)
                if sel:
                    dve.wait_ge(removed, 2 * k + 1)
                    dve.nop(nofuse=True)
                    find(k, par, 1, 0)
                if kk == CT + 1:
                    dispatch(0)
                if rou:
                    dve.wait_ge(el_ready, k - 1)
                    nc.vector.reciprocal(share[:], esum[:]).then_inc(share_a, 1)
                if sel:
                    dve.wait_ge(removed, 2 * k + 2)
                    dve.nop(nofuse=True)
                    find(k, par, 1, 1)
                if att:
                    dve.wait_ge(pv_mm, k)
                    den = ps_pv[:, :, 2 * HD:VW]
                    nc.vector.reciprocal(rden[:].rearrange("p (j h) -> p j h", h=2), den).then_inc(rden_ready, 1)
                if sel:
                    dve.wait_ge(found, 4 * k + 4)
                    nc.vector.scalar_tensor_tensor(cross[:], ranks[:, HEADS:2 * HEADS, :], -1.0, ranks[:, 0:HEADS, :],
                                                   ALU.mult, ALU.min).then_inc(crossed, 1)
                if rou:
                    dve.wait_ge(share_a, k - 1)
                    nc.vector.tensor_scalar(share_all[:, bass.ds(k - 2, 1)], share[:], tg[:, 1:2], None, ALU.mult
                                            ).then_inc(share_ready, 1)
                if att:
                    dve.wait_ge(rden_ready, k)
                    nc.vector.tensor_tensor(cn[:].rearrange("p (j h d) -> p j h d", h=2, d=HD),
                                            ps_pv[:, :, 0:2 * HD].rearrange("p j (h d) -> p j h d", h=2),
                                            rden[:].rearrange("p (j h) -> p j h", h=2).unsqueeze(3).to_broadcast([P, PAIRS, 2, HD]),
                                            ALU.mult).then_inc(cn_ready, 1)
                if nx:
                    low, high = s_sb[:, nxt, :, 0:HN], s_sb[:, nxt, :, HN:N]
                    dve.wait_ge(s_ready, k + 2)
                    if later(kk, -1, 1):
                        dve.wait_ge(negated, k + 1)
                    nc.vector.tensor_tensor(hi[:], low, high, ALU.max).then_inc(paired, 1)
                if sel:
                    dve.wait_ge(crossed, k + 1)
                    nc.vector.tensor_reduce(limit[:], cross[:], AX.X, ALU.max).then_inc(limit_ready, 1)
                if nx:
                    nc.vector.tensor_tensor(pairs[:, nxt, 0:HEADS, :], low, high, ALU.min).then_inc(paired, 1)
                if nx:
                    dve.wait_ge(paired, 2 * k + 3)
                    if later(kk, -1, 2):
                        dve.wait_ge(z_ready, k)
                    nc.vector.tensor_reduce(row_max[:, nxt], hi[:], AX.X, ALU.max).then_inc(max_ready, 1)
                if sel:
                    dve.wait_ge(limit_ready, k + 1)
                    if later(kk, 0, 2):
                        dve.wait_ge(p_mm, k - 1)
                    nc.vector.scalar_tensor_tensor(drop[:, par], s_sb[:, par], 0.0,
                                                   limit[:].unsqueeze(2).to_broadcast([P, HEADS, N]),
                                                   ALU.add, ALU.is_le, accum_out=count[:, 2:3]).then_inc(drop_ready, 1)
                if att:
                    dve.wait_ge(o_mm, k)
                    if kk == 1:
                        dve.wait_ge(gate_ready, 1)
                    x1 = x1_all[:, bass.ds(k - 1, 1), :].rearrange("p a d -> p (a d)")
                    nc.vector.scalar_tensor_tensor(x1, ps_o, tg[:, 0:1],
                                                   x_all[:, bass.ds(k - 1, 1), :].rearrange("p a d -> p (a d)"),
                                                   ALU.mult, ALU.add).then_inc(x1_ready, 1)
                if att:
                    dve.wait_ge(x1_ready, k)
                    dve.nop(nofuse=True)
                    nc.vector.bn_stats(stats2[:], x1).then_inc(st2_raw, 1)
                if att:
                    dve.wait_ge(st2_raw, k)
                    if later(kk, 1, 1):
                        dve.wait_ge(r2, k - 1)
                    dve.nop(nofuse=True)
                    nc.vector.bn_aggr(mv2[:], stats2[:]).then_inc(st2, 1)
                if kk == -1:
                    dve.wait_ge(consts_in, 16)
                    nc.vector.tensor_scalar(drop_id[:], ident, DROP, None, ALU.mult).then_inc(drop_id_set, 1)
                    nc.vector.tensor_copy(before[:], const[:, C_BEFORE:C_BEFORE + P]).then_inc(before_set, 1)

            ties = ctx.enter_context(dve.register("ties"))
            run(step, -2, TILES + 2)(dve)
            dve.wait_ge(chosen_ready, TILES)
            dispatch(1)
            dve.wait_ge(share_ready, TILES)
            combine(0)
            combine(1)

        @block.tensor
        def _(pe):
            def unit_rows(u, fronts):
                pe.wait_ge(xs_in[u.slot], u.uses * 16)
                pe.wait_ge(xs_ready, u.n + 2)
                pe.wait_ge(q_ready, fronts)
                nc.tensor.transpose(ps_xs, xs_ring[:, u.slot, :], ident).then_inc(xs_mm, 1)

            def unit_hidden(u):
                pe.wait_ge(w_in[u.slot], u.uses * 16)
                pe.wait_ge(h_ready, u.n + 3 - u.back)
                pe.wait_ge(xs_ready, u.n + 3)
                for c in range(FC):
                    last = nc.tensor.matmul(ps_h[u.bank][:, c, :], w_ring[:, u.slot, c * P:c * P + P],
                                            xs_t[:, u.par, :], start=True, stop=True)
                last.then_inc(h_mm, 1)

            def unit_out(u):
                pe.wait_ge(y_ready, u.n + 3 - u.back)
                pe.wait_ge(h_ready, u.n + 3)
                y = ps_y[u.bank]
                for c in range(FC):
                    nc.tensor.matmul(y, h_t[:, u.par, c, :], w_ring[:, u.slot, F + c * D:F + c * D + D],
                                     start=(c == 0), stop=False)
                nc.tensor.matmul(y, ones_row[:], w_ring[0:1, u.slot, 2 * F + FC:WW], start=False, stop=True).then_inc(y_mm, 1)

            def rank(ch):
                pe.wait_ge(chosen_ready, CT * (ch + 1))
                pe.wait_ge(before_set, 1)
                pe.wait_ge(q_ready, min(CT * (ch + 1) + 3, TILES))
                pe.wait_ge(xs_ready, 2 + ch * TILE_UNITS)
                own = chosen[:, ch * CT:ch * CT + CT, :]
                nc.tensor.matmul(ps_rank, before[:], own, start=True, stop=False)
                for tt in range(CT - 1):
                    left = CT - 1 - tt
                    nc.tensor.matmul(ps_rank[:, tt + 1:CT, :], ones_bf[:],
                                     own[:, tt:tt + 1, :].to_broadcast([P, left, E_N]), start=False, stop=(left == 1))
                for tt in range(CT):
                    last = nc.tensor.matmul(ps_total, ones_bf[:], own[:, tt, :], start=(tt == 0), stop=(tt == CT - 1))
                last.then_inc(rank_mm, 1)

            def step(k, par, kk, half, units):
                nxt = (par + 1) % 2
                att, rou = has(kk, 1), has(kk, 2)
                att_batch, next_batch = (half - 1 + par, half + par) if kk is None else ((kk - 1) // 2, (kk + 1) // 2)
                fronts = k + 2 if kk is None else min(kk + 2, TILES)
                u = units or [None, None]

                def scores(hh):
                    heads = slice(8 * hh, 8 * hh + 8)
                    mm = nc.tensor.matmul(ps_s[:, heads, :], q_t[:, nxt, :],
                                          kb[:, bass.ds(next_batch, 1), heads, :].rearrange("p a h n -> p (a h n)"),
                                          start=True, stop=True)
                    if hh == 1:
                        mm.then_inc(s_mm, 1)

                if u[0]:
                    unit_rows(u[0], fronts)
                if has(kk, -1):
                    pe.wait_ge(q_ready, k + 2)
                    pe.wait_ge(kb_ready, B if kk is None else next_batch + 1)
                    if later(kk, -1, 1):
                        pe.wait_ge(s_ready, k + 1)
                    scores(0)
                if rou:
                    pe.wait_ge(xn2_ready, k - 1)
                    pe.wait_ge(count_read, k if kk is None or kk <= TILES else TILES)
                    nc.tensor.transpose(ps_x2, xn2[:, par, :], ident).then_inc(x2_mm, 1)
                if has(kk, -1):
                    scores(1)
                if rou:
                    pe.wait_ge(x2_ready, k - 1)
                    nc.tensor.matmul(ps_l, xn2_t[:], wr[:], start=True, stop=True).then_inc(l_mm, 1)
                if att:
                    pe.wait_ge(drop_ok, k)
                    pe.wait_ge(z_ready, k)
                    if kk == 1:
                        pe.wait_ge(drop_id_set, 1)
                    if kk == 1:
                        pe.wait_ge(v_ready, 2)
                    if later(kk, 1, 1):
                        pe.wait_ge(pt_ready, k - 1)
                    for j in range(PAIRS):
                        nc.tensor.matmul(ps_p[:, j, :], z_sb[:, nxt, j, :], ident, start=True, stop=False, is_transpose=True)
                        last = nc.tensor.matmul(ps_p[:, j, :], drop[:, nxt, 2 * j:2 * j + 2, :].rearrange("p h n -> p (h n)"),
                                                drop_id[:], start=False, stop=True)
                    last.then_inc(p_mm, 1)
                if u[0]:
                    unit_hidden(u[0])
                if kk == CT + 1:
                    rank(0)
                if att:
                    pe.wait_ge(pt_ready, k)
                    if later(kk, 1, 1):
                        pe.wait_ge(idx_ready, k - 1)
                    for j in range(PAIRS):
                        last = nc.tensor.matmul(ps_pv[:, j, :], p_t[:, j, :],
                                                vb[:, bass.ds(att_batch, 1), j, :].rearrange("p a v -> p (a v)"),
                                                start=True, stop=True)
                    last.then_inc(pv_mm, 1)
                if u[1]:
                    unit_rows(u[1], fronts)
                if u[0]:
                    unit_out(u[0])
                if u[1]:
                    unit_hidden(u[1])
                if att:
                    pe.wait_ge(cn_ready, k)
                    nc.tensor.transpose(ps_c, cn[:], ident).then_inc(c_mm, 1)
                if att:
                    pe.wait_ge(ct_ready, k)
                    if kk == 1:
                        pe.wait_ge(w_late, 64)
                    nc.tensor.matmul(ps_o, c_t[:], wo[:], start=True, stop=False)
                    nc.tensor.matmul(ps_o, ones_row[:], bo_row[:], start=False, stop=True).then_inc(o_mm, 1)
                if has(kk, -2):
                    pe.wait_ge(xn_ready, k + 3)
                    if later(kk, -2, 1):
                        pe.wait_ge(q_ready, k + 2)
                    if units:
                        pe.wait_ge(xs_ready, units[-1].n + 3)
                    if kk == CT + 1:
                        pe.wait_ge(plan, PLACED)
                    nc.tensor.transpose(ps_xt, xn[:, par, :], ident).then_inc(xt_mm, 1)
                if has(kk, -2):
                    pe.wait_ge(xt_ready, k + 3)
                    if kk == -2:
                        pe.wait_ge(w_q, 32)
                    nc.tensor.matmul(ps_q, wq[:], xn_t[:, par, :], start=True, stop=True).then_inc(q_mm, 1)
                if u[1]:
                    unit_out(u[1])
                if has(kk, 0):
                    pe.wait_ge(drop_ready, k + 1)
                    if att:
                        pe.wait_ge(x1_ready, k)
                    nc.tensor.matmul(ps_count[:, 0:1], count[:, 2:3], ones_col[:], start=True, stop=True)
                    nc.tensor.matmul(ps_count[:, 1:2], count[:, 0:1], removed_weight[:], start=True, stop=False)
                    nc.tensor.matmul(ps_count[:, 1:2], count[:, 1:2], removed_weight[:], start=False, stop=True).then_inc(count_mm, 1)

                if kk == -1:
                    pe.wait_ge(w_v, 48)
                    pe.wait_ge(consts_set, 7)
                    for b in range(B):
                        nc.tensor.matmul(ps_p[:, b, :], ctx_twice[:, b].rearrange("p a n -> p (a n)"), wv[:], start=True, stop=False)
                        last = nc.tensor.matmul(ps_p[:, b, :], ones_row[:], bv_row[:], start=False, stop=True)
                    last.then_inc(v_mm, 1)

            pe.sem_inc(h_mm, 2)
            pe.sem_inc(y_mm, 2)
            pe.wait_ge(w_kv, 48)
            nc.tensor.matmul(ps_s[:, 0:8, :], wk[:], ctx_t[:], start=True, stop=True).then_inc(k_mm, 1)
            pe.wait_ge(consts_in, 16)
            run(step, -2, TILES + 2)(pe)

            rank(1)
            pe.wait_ge(plan, PLANS + PLACED)
            units_after(pe, lambda u: unit_rows(u, TILES), unit_hidden, unit_out)


def kernel(**inputs):
    import concourse.bacc as bacc
    from concourse.bass_utils import run_bass_kernel_spmd
    a = {n: np.asarray(v) for n, v in inputs.items()}
    L = "L0_xattn_"
    M = "L0_ffn_"
    const = np.zeros((P, C_W), np.float32)
    const[:, C_ID:C_ID + P] = np.eye(P, dtype=np.float32)
    const[np.arange(P), C_HM + np.arange(P) // HD] = 1.0
    const[:, C_IOTA:C_IOTA + E_N] = np.arange(E_N, dtype=np.float32)
    const[:, C_EDGE:C_EDGE + CT] = P * np.arange(CT)
    const[:, C_UPTO:C_UPTO + E_N * E_N] = np.tril(np.ones((E_N, E_N))).ravel()
    const[:, C_UNIT:C_UNIT + UNITS] = np.arange(UNITS)
    const[:, C_BEFORE:C_BEFORE + P] = np.triu(np.ones((P, P)), 1)
    c = a["ctx_1024"].transpose(2, 0, 1)
    arrays = {
        "x": a["x"].reshape(TILES, P, D).transpose(1, 0, 2),
        "const": const,
        "wq": a[L + "Wq"].T, "wk": a[L + "Wk"].T, "wv": a[L + "Wv"].T, "wo": a[L + "Wo"].T,
        "bq": a[L + "bq"].reshape(P, 1), "bk": a[L + "bk"].reshape(P, 1),
        "bv": a[L + "bv"].reshape(1, D), "bo": a[L + "bo"].reshape(1, D),
        "ctx": c,
        "gates": np.broadcast_to(np.concatenate([a["g_xattn"], a["g_ffn"]])[None, :], (P, 2)),
        "wr": a[M + "w_router"],
        "w": np.concatenate([
            a[M + "w1"],
            a[M + "w2"].reshape(E_N, FC, P, D).transpose(0, 2, 1, 3).reshape(E_N, P, F),
            a[M + "b1"].reshape(E_N, FC, P).transpose(0, 2, 1),
            np.broadcast_to(a[M + "b2"][:, None, :], (E_N, P, D)),
        ], axis=2),
    }
    nc = bacc.Bacc("TRN2", target_bir_lowering=False, num_devices=1)
    t, feed = {}, {}
    for n, v in arrays.items():
        v = np.ascontiguousarray(v)
        feed["in_" + n] = v
        t[n] = nc.dram_tensor("in_" + n, v.shape, F32, kind="ExternalInput").ap()
    out = nc.dram_tensor("out", (TILES, P, D), F32, kind="ExternalOutput").ap()
    t["out"] = out.rearrange("t p d -> p t d")
    for n in ("xs", "ys"):
        t[n] = [nc.dram_tensor(f"{n}{ch}", (UNITS * P, D), F32, kind="Internal").ap() for ch in range(CHUNKS)]
    build(nc, t)
    r = run_bass_kernel_spmd(nc, [feed], core_ids=[0])
    return r.results[0]["out"].reshape(B, S, D)
```

```python
import concourse.bass as bass
import numpy as np
from concourse import mybir
from contextlib import ExitStack

F32 = mybir.dt.float32
BF16 = mybir.dt.bfloat16
I32 = mybir.dt.int32
U32 = mybir.dt.uint32
ALU = mybir.AluOpType
ACT = mybir.ActivationFunctionType
AX = mybir.AxisListType

P = 128
B, S, D = 8, 256, 128
N = 64
HEADS = 16
HD = D // HEADS
TOPK = 32
E_N = 8
F = 512
FC = F // P
TILES = B * S // P
PAIRS = HEADS // 2
VW = 2 * HD + 2
SCALE = float(HD) ** -0.5
NEG = -3.0e38
DROP = -float(2 ** 100)
HN = N // 2
HALF = TOPK // 2
DROPPED = P * HEADS * (N - TOPK)
REMOVED = P * 2 * HEADS * 8
EPS = 1e-5

CHUNKS = 2
CT = TILES // CHUNKS
UNITS = CT + E_N - 1
BLOCKS = E_N * CT + UNITS - CT
RINGS = (4, 6)
PLACES = (range(0, 4), range(4, 10))
TURN_FIRST = 1
WW = 2 * F + FC + D

C_ID, C_HM, C_IOTA = 0, 128, 144
C_EDGE = C_IOTA + E_N
C_UPTO = C_EDGE + CT
C_UNIT = C_UPTO + E_N * E_N
C_BEFORE = C_UNIT + UNITS
C_BASE = C_BEFORE + P
C_W = C_BASE + E_N

LOOPS = ((4, 8), (10, 14))
FIRST_UNITS = 10


def build(nc, t):
    ctx = ExitStack()
    with ctx:
        def sb(name, shape, dt=F32):
            return ctx.enter_context(nc.sbuf_tensor(name, shape, dt))

        def ps(name, shape):
            return ctx.enter_context(nc.psum_tensor(name, shape, F32))

        def sem(name):
            return ctx.enter_context(nc.semaphore(name))

        x_all = sb("x_all", [P, TILES, D])
        const = sb("const", [P, C_W])
        ident = const[:, C_ID:C_ID + P]
        head_mask = const[:, C_HM:C_HM + HEADS]
        iota8 = const[:, C_IOTA:C_IOTA + E_N]
        edges = const[:, C_EDGE:C_EDGE + CT]
        upto_mask = const[:, C_UPTO:C_UPTO + E_N * E_N]
        unit_no = const[:, C_UNIT:C_UNIT + UNITS]
        ones_row = sb("ones_row", [1, P])
        ones_col = sb("ones_col", [P, 1])
        removed_weight = sb("removed_weight", [P, 1])
        less_dropped = sb("less_dropped", [1, 1])
        half_neg = sb("half_neg", [P, 1])
        lowest = sb("lowest", [P, 1])
        wq = sb("wq", [P, D])
        wk = sb("wk", [P, D])
        wv = sb("wv", [P, D])
        wo = sb("wo", [P, D])
        wr = sb("wr", [P, E_N])
        ctx_t = sb("ctx_t", [P, B, N])
        ctx_twice = sb("ctx_twice", [P, B, 2, N])
        bq = sb("bq", [P, 1])
        bk = sb("bk", [P, 1])
        bv_row = sb("bv_row", [1, D])
        bo_row = sb("bo_row", [1, D])
        gates = sb("gates", [P, 2])
        tg = sb("tg", [P, 2])
        k_t = sb("k_t", [P, B, N])
        kb = sb("kb", [P, B, HEADS, N])
        vb = sb("vb", [P, B, PAIRS, VW])
        stats = sb("stats", [P, 2, 6])
        mv = sb("mv", [P, 2, 2])
        rstd = sb("rstd", [P, 2, 3])
        xn = sb("xn", [P, 2, D])
        xn_t = sb("xn_t", [P, 2, P])
        q_t = sb("q_t", [P, 2, P])
        s_sb = sb("s_sb", [P, 2, HEADS, N])
        hi = sb("hi", [P, HEADS, HN])
        pairs = sb("pairs", [P, 2, 2 * HEADS, HN])
        rest = sb("rest", [P, 2 * HEADS, HN])
        ranks = sb("ranks", [P, 2 * HEADS, HALF])
        cross = sb("cross", [P, HEADS, HALF])
        limit = sb("limit", [P, HEADS])
        row_max = sb("row_max", [P, 2, HEADS])
        z_sb = sb("z_sb", [P, 2, PAIRS, P])
        drop = sb("drop", [P, 2, HEADS, N], BF16)
        top_mark = sb("top_mark", [P, 2 * HEADS, HN], BF16)
        count = sb("count", [P, 3])
        count_sq = sb("count_sq", [1, 2])
        count_off = sb("count_off", [1, 1])
        work = sb("work", [P, HEADS, N])
        work8 = sb("work8", [P, HEADS, 8])
        drop_id = sb("drop_id", [P, P], BF16)
        p_t = sb("p_t", [P, PAIRS, P])
        rden = sb("rden", [P, HEADS])
        cn = sb("cn", [P, D])
        c_t = sb("c_t", [P, P])
        x1_all = sb("x1_all", [P, TILES, D])
        stats2 = sb("stats2", [P, 6])
        mv2 = sb("mv2", [P, 2])
        rstd2 = sb("rstd2", [P, 3])
        xn2 = sb("xn2", [P, 2, D])
        xn2_t = sb("xn2_t", [P, P])
        top8 = sb("top8", [P, 8])
        idx8 = sb("idx8", [P, 8], U32)
        idxf = sb("idxf", [P, 1])
        dl = sb("dl", [P, 8])
        el = sb("el", [P, 8])
        esum = sb("esum", [P, 1])
        share = sb("share", [P, 1])
        share_all = sb("share_all", [P, TILES])
        chosen = sb("chosen", [P, TILES, E_N], BF16)
        before = sb("before", [P, P], BF16)
        ones_bf = sb("ones_bf", [P, P], BF16)
        full = sb("full", [P, E_N, CT])
        n_units = sb("n_units", [P, E_N])
        upto = sb("upto", [P, E_N, E_N])
        last_unit = sb("last_unit", [P, E_N])
        seen = sb("seen", [P, CHUNKS, E_N], BF16)
        base = sb("base", [1, E_N], BF16)
        slot_terms = sb("slot_terms", [P, E_N])
        slot_f = sb("slot_f", [P, 2])
        slot_now = sb("slot_now", [P, 2], U32)
        slot = sb("slot", [P, TILES])
        back = sb("back", [P, TILES], U32)
        moved = sb("moved", [P, E_N])
        moved_terms = sb("moved_terms", [P, CT, E_N])
        moved_own = sb("moved_own", [P, CT])
        past = sb("past", [1, UNITS, E_N])
        past_less = sb("past_less", [1, UNITS, E_N])
        less = sb("less", [P, E_N])
        block_f = sb("block_f", [1, UNITS])
        unit_block = sb("unit_block", [1, CHUNKS, UNITS], I32)
        zeros = sb("zeros", [P, D])
        w_ring = sb("w_ring", [P, sum(RINGS), WW])
        xs_ring = sb("xs_ring", [P, sum(RINGS), D])
        xs_t = sb("xs_t", [P, 2, P])
        h_t = sb("h_t", [P, 2, FC, P])
        y_all = sb("y_all", [P, 2 * UNITS, D])
        y_back = x_all[:].rearrange("p (c t) d -> p c t d", c=CHUNKS)

        ps_s = ps("ps_s", [P, HEADS, N])
        ps_p = ps("ps_p", [P, PAIRS, P])
        ps_h = [ps("ps_h", [P, FC, P]), ps_s[:, 0:HEADS // 2, :].rearrange("p (c q) n -> p c (q n)", c=FC)]
        ps_y = [ps("ps_y", [P, 512])[:, 0:D], ps_p[:, 0, :]]
        ps_front = ps("ps_front", [P, 512])
        ps_xt, ps_q, ps_xs = ps_front[:, 0:128], ps_front[:, 128:256], ps_front[:, 256:384]
        ps_rank = ps_front[:, 384:384 + E_N]
        ps_total = ps_front[:, 384 + E_N:384 + 2 * E_N]
        ps_att = ps("ps_att", [P, 512])
        ps_pv = ps_att[:, 0:PAIRS * VW].rearrange("p (j v) -> p j v", v=VW)
        ps_c = ps_x2 = ps_att[:, 144:272]
        ps_o = ps_att[:, 272:400]
        ps_l = ps_att[:, 400:408]
        ps_count = ps_att[0:1, 408:410]

        x_first, x_rest = sem("x_first"), sem("x_rest")
        w_q, w_kv, w_v, w_late, w_moe, consts_in = sem("w_q"), sem("w_kv"), sem("w_v"), sem("w_late"), sem("w_moe"), sem("consts_in")
        consts_set, gate_ready = sem("consts_set"), sem("gate_ready")
        k_mm, k_ready, kb_zero, kb_ready = sem("k_mm"), sem("k_ready"), sem("kb_zero"), sem("kb_ready")
        v_mm, vb_zero, v_ready = sem("v_mm"), sem("vb_zero"), sem("v_ready")
        st1_raw, st1, var1, rsq1, r1 = sem("st1_raw"), sem("st1"), sem("var1"), sem("rsq1"), sem("r1")
        xn_ready, xt_mm, xt_ready, q_mm, q_ready = sem("xn_ready"), sem("xt_mm"), sem("xt_ready"), sem("q_mm"), sem("q_ready")
        s_mm, s_ready = sem("s_mm"), sem("s_ready")
        paired, max_ready, negated = sem("paired"), sem("max_ready"), sem("negated")
        found, marked, penalised, removed = sem("found"), sem("marked"), sem("penalised"), sem("removed")
        crossed, limit_ready, drop_ready, z_ready = sem("crossed"), sem("limit_ready"), sem("drop_ready"), sem("z_ready")
        count_mm, count_read, drop_ok = sem("count_mm"), sem("count_read"), sem("drop_ok")
        drop_id_set, p_mm, pt_ready = sem("drop_id_set"), sem("p_mm"), sem("pt_ready")
        pv_mm, rden_ready, cn_ready, c_mm, ct_ready, o_mm = sem("pv_mm"), sem("rden_ready"), sem("cn_ready"), sem("c_mm"), sem("ct_ready"), sem("o_mm")
        x1_ready = sem("x1_ready")
        st2_raw, st2, var2, rsq2, r2 = sem("st2_raw"), sem("st2"), sem("var2"), sem("rsq2"), sem("r2")
        xn2_ready, x2_mm, x2_ready, l_mm = sem("xn2_ready"), sem("x2_mm"), sem("x2_ready"), sem("l_mm")
        top_ready, dl_ready, el_ready, idx_ready = sem("top_ready"), sem("dl_ready"), sem("el_ready"), sem("idx_ready")
        share_a, idxf_ready, share_ready, chosen_ready = sem("share_a"), sem("idxf_ready"), sem("share_ready"), sem("chosen_ready")
        moves, moved_ready, back_ready = sem("moves"), sem("moved_ready"), sem("back_ready")
        rank_mm, rank_read, total_read, plan = sem("rank_mm"), sem("rank_read"), sem("total_read"), sem("plan")
        seen_zero, seen_ready = sem("seen_zero"), sem("seen_ready")
        slot_ready, blocks_ready, cleared = sem("slot_ready"), sem("blocks_ready"), sem("cleared")
        scattered = [sem(f"scattered{par}") for par in range(2)]
        zeros_set, before_set = sem("zeros_set"), sem("before_set")
        w_in = [sem(f"w_in{i}") for i in range(sum(RINGS))]
        xs_in = [sem(f"xs_in{i}") for i in range(sum(RINGS))]
        xs_mm, xs_ready, h_mm, h_ready, y_mm, y_ready = (sem("xs_mm"), sem("xs_ready"), sem("h_mm"), sem("h_ready"),
                                                        sem("y_mm"), sem("y_ready"))
        out_ready, stored = sem("out_ready"), sem("stored")
        y_out = [sem(f"y_out{ch}") for ch in range(CHUNKS)]
        y_in = [[sem(f"y_in{ch}_{tt}") for tt in range(CT)] for ch in range(CHUNKS)]

        block = ctx.enter_context(nc.Block())

        class Unit:
            def __init__(self, chunk, turn, r, even=0):
                self.chunk, self.slot, self.uses = chunk, PLACES[chunk][r], turn + 1
                self.j = turn * RINGS[chunk] + r
                self.n = self.j + chunk * UNITS
                self.par = even if type(turn) is not int else self.n % 2
                beside_tiles = chunk == 0 and (type(turn) is not int or self.n < UNITS)
                self.bank, self.back = (0, 1) if beside_tiles else (self.par, 2)

        def unit(chunk, j):
            return Unit(chunk, j // RINGS[chunk], j % RINGS[chunk])

        def run(step_of, first, last):
            def go(eng):
                def peeled(k):
                    j = 2 * (k - FIRST_UNITS)
                    js = range(j, min(j + 2, UNITS)) if FIRST_UNITS <= k else ()
                    step_of(k, k % 2, k, k // 2, [unit(0, j) for j in js])

                k = first
                for a, b in LOOPS:
                    for k in range(k, min(a, last)):
                        peeled(k)
                    with eng.Fori(a // 2, b // 2) as i:
                        for par in range(2):
                            cs = range(2 * (par - FIRST_UNITS), 2 * (par - FIRST_UNITS) + 2) if a >= FIRST_UNITS else ()
                            step_of(i * 2 + par, par, None, i,
                                    [Unit(0, i + c // RINGS[0], c % RINGS[0], c % 2) for c in cs])
                    k = b
                for k in range(k, last):
                    peeled(k)
            return go

        def units_after(eng, rows, hidden, out):
            first = [unit(1, j) for j in range(TURN_FIRST)]
            last = [unit(1, j) for j in range(TURN_FIRST + 2 * RINGS[1], UNITS)]

            def three(u):
                rows(u[2])
                hidden(u[1])
                out(u[0])
            ahead = [unit(1, TURN_FIRST + i) for i in range(2)]
            rows((first + ahead)[0])
            rows((first + ahead)[1])
            hidden((first + ahead)[0])
            for i in range(len(first)):
                three((first + ahead)[i:i + 3])
            with eng.Fori(0, 2) as i:
                for r in range(TURN_FIRST, TURN_FIRST + RINGS[1]):
                    three([Unit(1, i + (r + d) // RINGS[1], (r + d) % RINGS[1], (r + d + UNITS) % 2) for d in range(3)])
            for i in range(len(last) - 2):
                three(last[i:i + 3])
            hidden(last[-1])
            out(last[-2])
            out(last[-1])

        def has(k, lag):
            return k is None or 0 <= k - lag < TILES

        def chunk_of_router(k, kk):
            return int(k.max_val >= FIRST_UNITS) if kk is None else int(kk >= FIRST_UNITS)

        def later(k, lag, n):
            return k is None or k - lag >= n


        @block.sync
        def _(sp):
            sp.dma_start(x_all[:, 0:2, :], t["x"][:, 0:2, :]).then_inc(x_first, 16)
            sp.dma_start(const[:], t["const"]).then_inc(consts_in, 16)
            sp.dma_start(wq[:], t["wq"]).then_inc(w_q, 16)
            sp.dma_start(bq[:], t["bq"]).then_inc(w_q, 16)
            sp.wait_ge(k_ready, 1)
            sp.dma_start(x_all[:, 2:TILES, :], t["x"][:, 2:TILES, :]).then_inc(x_rest, 16)
            sp.wait_ge(zeros_set, 1)
            sp.wait_ge(s_ready, 1)
            for ch in range(CHUNKS):
                sp.dma_start(t["xs"][ch].rearrange("(j p) d -> p j d", p=P),
                             zeros[:].unsqueeze(1).to_broadcast([P, BLOCKS, D])).then_inc(cleared, 16)

            def unit_at(u):
                return sp.value_load(unit_block[0:1, u.chunk, bass.ds(u.j, 1)], min_val=0, max_val=BLOCKS - 1)

            def load_weights(u, block):
                e = nc.s_assert_within(block // CT - block // (E_N * CT), min_val=0, max_val=E_N - 1)
                sp.dma_start(w_ring[:, u.slot, :], t["w"][bass.ds(e, 1), :, :].rearrange("a p n -> (a p) n")
                             ).then_inc(w_in[u.slot], 16)

            def load_rows(u, block):
                sp.dma_start(xs_ring[:, u.slot, :], t["xs"][u.chunk][bass.ds(block * P, P), :]).then_inc(xs_in[u.slot], 16)

            def first_loads(ch):
                sp.wait_ge(blocks_ready, ch + 1)
                block = unit_at(unit(ch, 0))
                load_weights(unit(ch, 0), block)
                for par in range(2):
                    sp.wait_ge(scattered[par], 16 * CT // 2 * (ch + 1))
                load_rows(unit(ch, 0), block)
                for r in range(1, RINGS[ch]):
                    block = unit_at(unit(ch, r))
                    load_rows(unit(ch, r), block)
                    load_weights(unit(ch, r), block)

            def load_ahead(u, ahead):
                block = unit_at(ahead)
                sp.wait_ge(y_ready, u.n + 3)
                load_rows(ahead, block)
                load_weights(ahead, block)

            def store(u, number):
                sp.wait_ge(y_ready, u.n + 2 + number)
                sp.dma_start(t["ys"][u.chunk][bass.ds(u.j * P, number * P), :].rearrange("(a p) d -> p a d", p=P),
                             y_all[:, bass.ds(u.n, number), :]).then_inc(y_out[u.chunk], 16)

            def loads_ahead(ch):
                ring = RINGS[ch]
                turns = (UNITS - ring) // ring
                with sp.Fori(0, turns) as i:
                    for r in range(ring):
                        load_ahead(Unit(ch, i, r), Unit(ch, i + 1, r))
                        if r % 2:
                            store(Unit(ch, i, r - 1), 2)
                for j in range(turns * ring, UNITS):
                    if j + ring < UNITS:
                        load_ahead(unit(ch, j), unit(ch, j + ring))
                    if j % 2:
                        store(unit(ch, j - 1), 2)

            first_loads(0)
            loads_ahead(0)
            first_loads(1)
            store(unit(0, UNITS - 1), 1)
            loads_ahead(1)
            store(unit(1, UNITS - 1), 1)
            for ch in range(CHUNKS):
                for tt in range(0, CT, 2):
                    sp.wait_ge(out_ready, ch * CT + tt + 2)
                    sp.dma_start(t["out"][:, ch * CT + tt:ch * CT + tt + 2, :], y_back[:, ch, tt:tt + 2, :]).then_inc(stored, 16)
            sp.wait_ge(stored, 16 * TILES // 2)

        @block.gpsimd
        def _(pool):
            nc.gpsimd.memset(zeros[:], 0.0).then_inc(zeros_set, 1)
            nc.gpsimd.memset(ones_row[:], 1.0).then_inc(consts_set, 1)
            nc.gpsimd.memset(half_neg[:], -0.5).then_inc(consts_set, 1)
            nc.gpsimd.memset(ones_col[:], 1.0).then_inc(consts_set, 1)
            nc.gpsimd.memset(ones_bf[:], 1.0).then_inc(consts_set, 1)
            nc.gpsimd.memset(lowest[:], NEG).then_inc(consts_set, 1)
            nc.gpsimd.memset(removed_weight[:], DROPPED / REMOVED).then_inc(consts_set, 1)
            nc.gpsimd.memset(less_dropped[:], -float(DROPPED)).then_inc(consts_set, 1)
            nc.gpsimd.memset(seen[:], 0.0).then_inc(seen_zero, 1)
            nc.gpsimd.memset(vb[:], 0.0).then_inc(vb_zero, 1)
            pool.wait_ge(vb_zero, 1)
            nc.gpsimd.memset(vb[0:64, :, :, 2 * HD:2 * HD + 1], 1.0).then_inc(vb_zero, 1)
            nc.gpsimd.memset(vb[64:128, :, :, 2 * HD + 1:VW], 1.0).then_inc(vb_zero, 1)
            pool.wait_ge(consts_in, 16)
            pool.wait_ge(consts_set, 7)
            pool.wait_ge(vb_zero, 3)
            pool.wait_ge(seen_zero, 1)

            def rsqrt(st_sem, var_sem, rsq_sem, r_sem, mv_, r_, n):
                pool.wait_ge(st_sem, n + 1)
                pool.nop(nofuse=True)
                nc.gpsimd.tensor_scalar(r_[:, 2:3], mv_[:, 1:2], EPS, None, ALU.add).then_inc(var_sem, 1)
                pool.wait_ge(var_sem, n + 1)
                nc.gpsimd.tensor_tensor(r_[:, 0:1], r_[:, 2:3], half_neg[:], ALU.pow).then_inc(rsq_sem, 1)
                pool.wait_ge(rsq_sem, n + 1)
                pool.nop(nofuse=True)
                nc.gpsimd.tensor_scalar(r_[:, 1:2], mv_[:, 0:1], r_[:, 0:1], -1.0, ALU.mult, ALU.mult).then_inc(r_sem, 1)

            def spread_keys(b):
                nc.gpsimd.tensor_tensor(kb[:, b, :, :], k_t[:, b, :].unsqueeze(1).to_broadcast([P, HEADS, N]),
                                        head_mask.unsqueeze(2).to_broadcast([P, HEADS, N]),
                                        ALU.mult).then_inc(kb_ready, 1)

            def scatter(k, par, kk, half):
                ch = chunk_of_router(k, kk)
                if kk == 2:
                    pool.wait_ge(cleared, 16 * CHUNKS)
                pool.wait_ge(rank_read, k - 1)
                pool.nop(nofuse=True)
                nc.gpsimd.tensor_copy(slot_now[:, par:par + 1], slot_f[:, par:par + 1]).then_inc(slot_ready, 1)
                nc.gpsimd.tensor_copy(slot[:, bass.ds(k - 2, 1)], slot_f[:, par:par + 1]).then_inc(slot_ready, 1)
                nc.gpsimd.tensor_tensor(seen[:, ch, :], seen[:, ch, :],
                                        chosen[:, bass.ds(k - 2, 1), :].rearrange("p a e -> p (a e)"), ALU.add
                                        ).then_inc(seen_ready, 1)
                pool.wait_ge(slot_ready, 2 * k - 2)
                pool.nop(nofuse=True)
                nc.gpsimd.indirect_dma_start(t["xs"][ch], bass.IndirectOffsetOnAxis(slot_now[:, par:par + 1], 0),
                                             xn2[:, par, :], None).then_inc(scattered[par], 16)

            def gather(ch):
                pool.wait_ge(back_ready, ch + 1)
                pool.wait_ge(y_out[ch], 16 * ((UNITS + 1) // 2))
                for tt in range(CT):
                    nc.gpsimd.indirect_dma_start(
                        y_back[:, ch, tt, :], None, t["ys"][ch],
                        bass.IndirectOffsetOnAxis(back[:, ch * CT + tt:ch * CT + tt + 1], 0)).then_inc(y_in[ch][tt], 16)

            def take_out(k, par, side):
                rows = slice(side * HEADS, side * HEADS + HEADS)
                pool.wait_ge(marked, 2 * k + 1 + side)
                pool.nop(nofuse=True)
                nc.gpsimd.tensor_tensor(rest[:, rows, :], top_mark[:, rows, :], lowest[:].unsqueeze(2).to_broadcast([P, HEADS, HN]),
                                        ALU.mult).then_inc(penalised, 1)
                pool.wait_ge(penalised, 2 * k + 1 + side)
                nc.gpsimd.tensor_tensor(rest[:, rows, :], rest[:, rows, :], pairs[:, par, rows, :], ALU.add).then_inc(removed, 1)

            def step(k, par, kk, half, units):
                if has(kk, 0):
                    take_out(k, par, 0)
                    take_out(k, par, 1)
                if has(kk, -2):
                    rsqrt(st1, var1, rsq1, r1, mv[:, par, :], rstd[:, par, :], k + 2)
                if kk == CT + 1:
                    scatter(k, par, kk, half)
                if kk is not None:
                    if kk == -2:
                        pool.wait_ge(k_ready, 1)
                    for b in range(2 * kk + 3, min(2 * kk + 5, B)) if kk > -2 else (0,):
                        spread_keys(b)
                if has(kk, 0):
                    pool.wait_ge(max_ready, k + 1)
                    if later(kk, 0, 2):
                        pool.wait_ge(p_mm, k - 1)
                    nc.gpsimd.tensor_tensor(z_sb[:, par].rearrange("p j (h n) -> p (j h) n", h=2), s_sb[:, par],
                                            row_max[:, par].unsqueeze(2).to_broadcast([P, HEADS, N]),
                                            ALU.subtract).then_inc(z_ready, 1)
                if has(kk, 1):
                    rsqrt(st2, var2, rsq2, r2, mv2[:], rstd2[:], k - 1)
                if has(kk, 2) and kk != CT + 1:
                    scatter(k, par, kk, half)
            run(step, -2, TILES + 2)(pool)
            gather(0)
            gather(1)

        @block.scalar
        def _(act):
            act.dma_start(wk[:], t["wk"]).then_inc(w_kv, 16)
            act.dma_start(ctx_t[:], t["ctx"]).then_inc(w_kv, 16)
            act.dma_start(bk[:], t["bk"]).then_inc(w_kv, 16)
            act.dma_start(ctx_twice[:], t["ctx"].unsqueeze(2).to_broadcast([P, B, 2, N])).then_inc(w_v, 16)
            act.dma_start(wv[:], t["wv"]).then_inc(w_v, 16)
            act.dma_start(bv_row[:], t["bv"]).then_inc(w_v, 16)
            act.dma_start(gates[:], t["gates"]).then_inc(w_late, 16)
            act.dma_start(wo[:], t["wo"]).then_inc(w_late, 16)
            act.dma_start(bo_row[:], t["bo"]).then_inc(w_late, 16)
            act.dma_start(wr[:], t["wr"]).then_inc(w_late, 16)
            for free_two in (xs_ready, h_ready, y_ready):
                act.sem_inc(free_two, 2)

            def norm(xin, r_, out, r_sem, n, out_sem):
                act.wait_ge(r_sem, n + 1)
                nc.scalar.activation(out, xin, ACT.Identity, scale=r_[:, 0:1], bias=r_[:, 1:2]).then_inc(out_sem, 1)

            def unit_rows(u):
                act.wait_ge(xs_mm, u.n + 1)
                act.wait_ge(h_mm, u.n + 1)
                nc.scalar.activation(xs_t[:, u.par, :], ps_xs, ACT.Copy).then_inc(xs_ready, 1)

            def unit_hidden(u):
                act.wait_ge(h_mm, u.n + 3)
                act.wait_ge(y_mm, u.n + 1)
                for c in range(FC):
                    last = nc.scalar.activation(h_t[:, u.par, c, :], ps_h[u.bank][:, c, :], ACT.Relu,
                                                bias=w_ring[:, u.slot, 2 * F + c:2 * F + c + 1])
                last.then_inc(h_ready, 1)

            def unit_out(u):
                act.wait_ge(y_mm, u.n + 3)
                nc.scalar.activation(y_all[:, bass.ds(u.n, 1), :].rearrange("p a d -> p (a d)"), ps_y[u.bank], ACT.Copy
                                     ).then_inc(y_ready, 1)

            def step(k, par, kk, half, units):
                nxt = (par + 1) % 2
                sel, att, rou = has(kk, 0), has(kk, 1), has(kk, 2)
                u = (units + [None, None])[:2]
                if u[0]:
                    unit_rows(u[0])
                if rou:
                    if later(kk, 2, 2):
                        act.wait_ge(scattered[par], 16 * (half - 1))
                    norm(x1_all[:, bass.ds(k - 2, 1), :], rstd2, xn2[:, par, :], r2, k - 2, xn2_ready)
                if rou:
                    act.wait_ge(x2_mm, k - 1)
                    nc.scalar.activation(xn2_t[:], ps_x2, ACT.Copy).then_inc(x2_ready, 1)
                if has(kk, -1):
                    act.wait_ge(s_mm, k + 2)
                    if later(kk, -1, 2):
                        act.wait_ge(z_ready, k)
                        act.wait_ge(drop_ok, k)
                    nc.scalar.activation(s_sb[:, nxt], ps_s[:], ACT.Copy).then_inc(s_ready, 1)
                if att:
                    act.wait_ge(p_mm, k)
                    if later(kk, 1, 1):
                        act.wait_ge(pv_mm, k - 1)
                    nc.scalar.activation(p_t[:], ps_p[:], ACT.Exp, scale=SCALE).then_inc(pt_ready, 1)
                if u[0]:
                    unit_hidden(u[0])
                if rou:
                    act.wait_ge(dl_ready, k - 1)
                    nc.scalar.activation(el[:], dl[:], ACT.Exp, accum_out=esum[:]).then_inc(el_ready, 1)
                if u[1]:
                    unit_rows(u[1])
                if u[0]:
                    unit_out(u[0])
                if u[1]:
                    unit_hidden(u[1])
                if att:
                    act.wait_ge(c_mm, k)
                    if later(kk, 1, 1):
                        act.wait_ge(o_mm, k - 1)
                    nc.scalar.activation(c_t[:], ps_c, ACT.Copy).then_inc(ct_ready, 1)
                if has(kk, -2):
                    norm(x_all[:, bass.ds(k + 2, 1), :], rstd[:, par, :], xn[:, par, :], r1, k + 2, xn_ready)
                if kk == -2:
                    act.wait_ge(w_kv, 48)
                    act.wait_ge(k_mm, 1)
                    nc.scalar.activation(k_t[:], ps_s[:, 0:8, :], ACT.Identity, bias=bk[:]).then_inc(k_ready, 1)
                if has(kk, -2):
                    act.wait_ge(xt_mm, k + 3)
                    nc.scalar.activation(xn_t[:, par, :], ps_xt, ACT.Copy).then_inc(xt_ready, 1)
                if has(kk, -2):
                    if kk == -2:
                        act.wait_ge(w_q, 32)
                    act.wait_ge(q_mm, k + 3)
                    nc.scalar.activation(q_t[:, par, :], ps_q, ACT.Identity, bias=bq[:]).then_inc(q_ready, 1)
                if has(kk, -1):
                    act.wait_ge(paired, 2 * k + 3)
                    if later(kk, -1, 2):
                        act.wait_ge(removed, 2 * k)
                    nc.scalar.activation(pairs[:, nxt, HEADS:2 * HEADS, :], hi[:], ACT.Copy, scale=-1.0).then_inc(negated, 1)
                if u[1]:
                    unit_out(u[1])
                if sel:
                    act.wait_ge(count_mm, k + 1)
                    if later(kk, 0, 1):
                        act.wait_ge(drop_ok, k)
                    nc.scalar.activation(count_sq[:], ps_count, ACT.Square, bias=less_dropped[:], accum_out=count_off[:]
                                         ).then_inc(count_read, 1)
                if kk == -1:
                    act.wait_ge(v_mm, 1)
                    act.wait_ge(vb_zero, 3)
                    for hh in range(2):
                        rows = slice(64 * hh, 64 * hh + 64)
                        src = ps_p[rows, :, :].rearrange("p b (j h d) -> p b j h d", h=2, d=HD)[:, :, :, hh, :]
                        nc.scalar.activation(vb[rows, :, :, hh * HD:hh * HD + HD], src, ACT.Copy).then_inc(v_ready, 1)
                    act.wait_ge(w_late, 64)
                    nc.scalar.activation(tg[:], gates[:], ACT.Tanh).then_inc(gate_ready, 1)

            run(step, -2, TILES + 2)(act)

            units_after(act, unit_rows, unit_hidden, unit_out)

        @block.vector
        def _(dve):
            def find(k, par, r, side):
                src = rest[:] if r else pairs[:, par]
                for g in range(side * HEADS, side * HEADS + HEADS):
                    last = nc.vector.max(ranks[:, g, 8 * r:8 * r + 8], src[:, g, :])
                last.then_inc(found, 1)

            def mark(k, par, side):
                rows = slice(side * HEADS, side * HEADS + HEADS)
                dve.wait_ge(found, 4 * k + 1 + side)
                if side == 0 and later(k if type(k) is int else None, 0, 1):
                    dve.wait_ge(count_mm, k)
                nc.vector.scalar_tensor_tensor(top_mark[:, rows, :], pairs[:, par, rows, :], 0.0,
                                               ranks[:, rows, 7:8].to_broadcast([P, HEADS, HN]),
                                               ALU.add, ALU.is_ge, accum_out=count[:, side:side + 1]).then_inc(marked, 1)

            def drop_exactly(par):
                dve.drain()
                nc.vector.tensor_copy(work[:], s_sb[:, par])
                with dve.Fori(0, TOPK // 8):
                    dve.drain()
                    for h in range(HEADS):
                        nc.vector.max(work8[:, h, :], work[:, h, :])
                    dve.drain()
                    for h in range(HEADS):
                        nc.vector.match_replace(work[:, h, :], work8[:, h, :], work[:, h, :], NEG)
                dve.drain()
                nc.vector.tensor_scalar(drop[:, par], work[:], NEG, None, ALU.is_gt)
                dve.drain()

            def check_ties(k, par, kk):
                if not has(kk, 1):
                    return
                nxt = (par + 1) % 2
                dve.wait_ge(count_read, k)
                dve.nop(nofuse=True)
                dve.reg_load(ties, count_off[:].bitcast(I32))
                with dve.If_ne(ties, 0):
                    drop_exactly(nxt)
                dve.sem_inc(drop_ok, 1)

            def slots(k, par, kk):
                dve.wait_ge(rank_mm, k - 1)
                if later(kk, 2, 2):
                    dve.wait_ge(slot_ready, 2 * k - 6)
                nc.vector.scalar_tensor_tensor(slot_terms[:], ps_rank, 1.0,
                                               chosen[:, bass.ds(k - 2, 1), :].rearrange("p a e -> p (a e)"),
                                               ALU.mult, ALU.mult, accum_out=slot_f[:, par:par + 1]).then_inc(rank_read, 1)

            def dispatch(ch):
                p0 = 7 * ch + 1
                dve.wait_ge(rank_mm, CT * (ch + 1))
                nc.vector.tensor_tensor(full[:], ps_total.unsqueeze(2).to_broadcast([P, E_N, CT]),
                                        edges.unsqueeze(1).to_broadcast([P, E_N, CT]), ALU.is_gt).then_inc(total_read, 1)
                dve.wait_ge(total_read, ch + 1)
                nc.vector.tensor_reduce(n_units[:], full[:], AX.X, ALU.add).then_inc(plan, 1)
                dve.wait_ge(plan, p0)
                nc.vector.tensor_tensor(upto[:], n_units[:].unsqueeze(1).to_broadcast([P, E_N, E_N]),
                                        upto_mask.rearrange("p (a b) -> p a b", b=E_N), ALU.mult).then_inc(plan, 1)
                nc.vector.tensor_scalar(less[:], n_units[:], -1.0, float(CT), ALU.mult, ALU.add).then_inc(plan, 1)
                dve.wait_ge(plan, p0 + 1)
                nc.vector.tensor_reduce(last_unit[:], upto[:], AX.X, ALU.add).then_inc(plan, 1)
                dve.wait_ge(plan, p0 + 3)
                nc.vector.tensor_tensor(past[:], last_unit[0:1, :].unsqueeze(1).to_broadcast([1, UNITS, E_N]),
                                        unit_no[0:1, :].unsqueeze(2).to_broadcast([1, UNITS, E_N]), ALU.is_le).then_inc(plan, 1)
                dve.wait_ge(plan, p0 + 4)
                nc.vector.tensor_tensor(past_less[:], past[:], less[0:1, :].unsqueeze(1).to_broadcast([1, UNITS, E_N]), ALU.mult
                                        ).then_inc(plan, 1)
                dve.wait_ge(plan, p0 + 5)
                nc.vector.tensor_reduce(block_f[:], past_less[:], AX.X, ALU.add).then_inc(plan, 1)
                dve.wait_ge(plan, p0 + 6)
                nc.vector.tensor_tensor(unit_block[:, ch, :], block_f[:], unit_no[0:1, :], ALU.add).then_inc(blocks_ready, 1)

            def units_places(ch):
                p0 = 3 * ch + 1
                own = slice(ch * CT, ch * CT + CT)
                nc.vector.scalar_tensor_tensor(moved[:], iota8, -float(CT), last_unit[:], ALU.mult, ALU.add).then_inc(moves, 1)
                dve.wait_ge(moves, p0)
                nc.vector.tensor_tensor(moved[:], moved[:], n_units[:], ALU.subtract).then_inc(moves, 1)
                dve.wait_ge(moves, p0 + 1)
                nc.vector.tensor_tensor(moved_terms[:], moved[:].unsqueeze(1).to_broadcast([P, CT, E_N]), chosen[:, own, :],
                                        ALU.mult).then_inc(moves, 1)
                dve.wait_ge(moves, p0 + 2)
                nc.vector.tensor_reduce(moved_own[:], moved_terms[:], AX.X, ALU.add).then_inc(moved_ready, 1)
                dve.wait_ge(moved_ready, ch + 1)
                dve.wait_ge(slot_ready, 2 * CT * (ch + 1))
                nc.vector.scalar_tensor_tensor(back[:, own], moved_own[:], float(P), slot[:, own], ALU.mult, ALU.add
                                               ).then_inc(back_ready, 1)

            def combine(ch):
                for tt in range(CT):
                    tile = ch * CT + tt
                    dve.wait_ge(y_in[ch][tt], 16)
                    nc.vector.scalar_tensor_tensor(y_back[:, ch, tt, :], y_back[:, ch, tt, :], share_all[:, tile:tile + 1],
                                                   x1_all[:, tile, :], ALU.mult, ALU.add).then_inc(out_ready, 1)

            def step(k, par, kk, half, units):
                nxt = (par + 1) % 2
                sel, att, rou, fr, nx = has(kk, 0), has(kk, 1), has(kk, 2), has(kk, -2), has(kk, -1)
                if sel:
                    dve.wait_ge(paired, 2 * k + 2)
                    dve.nop(nofuse=True)
                    find(k, par, 0, 0)
                check_ties(k, par, kk)
                if sel:
                    mark(k, par, 0)
                    dve.wait_ge(negated, k + 1)
                    dve.nop(nofuse=True)
                    find(k, par, 0, 1)
                if rou:
                    dve.wait_ge(l_mm, k - 1)
                    dve.nop(nofuse=True)
                    nc.vector.max(top8[:], ps_l).then_inc(top_ready, 1)
                if sel:
                    mark(k, par, 1)
                if rou:
                    dve.wait_ge(top_ready, k - 1)
                    nc.vector.tensor_scalar(dl[:], top8[:], top8[:, 0:1], None, ALU.subtract).then_inc(dl_ready, 1)
                    nc.vector.max_index(idx8[:], top8[:], ps_l).then_inc(idx_ready, 1)
                if fr:
                    if kk == -2:
                        dve.wait_ge(x_first, 16)
                    if kk == 0:
                        dve.wait_ge(x_rest, 16)
                    if later(kk, -2, 2):
                        dve.wait_ge(r1, k + 1)
                    nc.vector.bn_stats(stats[:, par, :], x_all[:, bass.ds(k + 2, 1), :].rearrange("p a d -> p (a d)")
                                       ).then_inc(st1_raw, 1)
                if rou:
                    dve.wait_ge(idx_ready, k - 1)
                    nc.vector.tensor_copy(idxf[:], idx8[:, 0:1]).then_inc(idxf_ready, 1)
                if fr:
                    dve.wait_ge(st1_raw, k + 3)
                    dve.nop(nofuse=True)
                    nc.vector.bn_aggr(mv[:, par, :], stats[:, par, :]).then_inc(st1, 1)
                if rou:
                    dve.wait_ge(idxf_ready, k - 1)
                    nc.vector.tensor_scalar(chosen[:, bass.ds(k - 2, 1), :].rearrange("p a e -> p (a e)"), iota8, idxf[:],
                                            None, ALU.is_equal).then_inc(chosen_ready, 1)
                if sel:
                    dve.wait_ge(removed, 2 * k + 1)
                    dve.nop(nofuse=True)
                    find(k, par, 1, 0)
                if kk in (CT + 1, TILES + 1):
                    slots(k, par, kk)
                    dispatch(kk // CT - 1)
                if rou:
                    dve.wait_ge(el_ready, k - 1)
                    nc.vector.reciprocal(share[:], esum[:]).then_inc(share_a, 1)
                if sel:
                    dve.wait_ge(removed, 2 * k + 2)
                    dve.nop(nofuse=True)
                    find(k, par, 1, 1)
                if att:
                    dve.wait_ge(pv_mm, k)
                    den = ps_pv[:, :, 2 * HD:VW]
                    nc.vector.reciprocal(rden[:].rearrange("p (j h) -> p j h", h=2), den).then_inc(rden_ready, 1)
                if sel:
                    dve.wait_ge(found, 4 * k + 4)
                    nc.vector.scalar_tensor_tensor(cross[:], ranks[:, HEADS:2 * HEADS, :], -1.0, ranks[:, 0:HEADS, :],
                                                   ALU.mult, ALU.min).then_inc(crossed, 1)
                if rou:
                    dve.wait_ge(share_a, k - 1)
                    nc.vector.tensor_scalar(share_all[:, bass.ds(k - 2, 1)], share[:], tg[:, 1:2], None, ALU.mult
                                            ).then_inc(share_ready, 1)
                if att:
                    dve.wait_ge(rden_ready, k)
                    nc.vector.tensor_tensor(cn[:].rearrange("p (j h d) -> p j h d", h=2, d=HD),
                                            ps_pv[:, :, 0:2 * HD].rearrange("p j (h d) -> p j h d", h=2),
                                            rden[:].rearrange("p (j h) -> p j h", h=2).unsqueeze(3).to_broadcast([P, PAIRS, 2, HD]),
                                            ALU.mult).then_inc(cn_ready, 1)
                if nx:
                    low, high = s_sb[:, nxt, :, 0:HN], s_sb[:, nxt, :, HN:N]
                    dve.wait_ge(s_ready, k + 2)
                    if later(kk, -1, 1):
                        dve.wait_ge(negated, k + 1)
                    nc.vector.tensor_tensor(hi[:], low, high, ALU.max).then_inc(paired, 1)
                if sel:
                    dve.wait_ge(crossed, k + 1)
                    nc.vector.tensor_reduce(limit[:], cross[:], AX.X, ALU.max).then_inc(limit_ready, 1)
                if nx:
                    nc.vector.tensor_tensor(pairs[:, nxt, 0:HEADS, :], low, high, ALU.min).then_inc(paired, 1)
                if nx:
                    dve.wait_ge(paired, 2 * k + 3)
                    if later(kk, -1, 2):
                        dve.wait_ge(z_ready, k)
                    nc.vector.tensor_reduce(row_max[:, nxt], hi[:], AX.X, ALU.max).then_inc(max_ready, 1)
                if sel:
                    dve.wait_ge(limit_ready, k + 1)
                    if later(kk, 0, 2):
                        dve.wait_ge(p_mm, k - 1)
                    nc.vector.scalar_tensor_tensor(drop[:, par], s_sb[:, par], 0.0,
                                                   limit[:].unsqueeze(2).to_broadcast([P, HEADS, N]),
                                                   ALU.add, ALU.is_le, accum_out=count[:, 2:3]).then_inc(drop_ready, 1)
                if att:
                    dve.wait_ge(o_mm, k)
                    if kk == 1:
                        dve.wait_ge(gate_ready, 1)
                    x1 = x1_all[:, bass.ds(k - 1, 1), :].rearrange("p a d -> p (a d)")
                    nc.vector.scalar_tensor_tensor(x1, ps_o, tg[:, 0:1],
                                                   x_all[:, bass.ds(k - 1, 1), :].rearrange("p a d -> p (a d)"),
                                                   ALU.mult, ALU.add).then_inc(x1_ready, 1)
                if att:
                    dve.wait_ge(x1_ready, k)
                    dve.nop(nofuse=True)
                    nc.vector.bn_stats(stats2[:], x1).then_inc(st2_raw, 1)
                if att:
                    dve.wait_ge(st2_raw, k)
                    if later(kk, 1, 1):
                        dve.wait_ge(r2, k - 1)
                    dve.nop(nofuse=True)
                    nc.vector.bn_aggr(mv2[:], stats2[:]).then_inc(st2, 1)
                if rou and kk not in (CT + 1, TILES + 1):
                    slots(k, par, kk)
                if kk in (CT + 1, TILES + 1):
                    units_places(kk // CT - 1)
                if kk == -1:
                    dve.wait_ge(consts_in, 16)
                    nc.vector.tensor_scalar(drop_id[:], ident, DROP, None, ALU.mult).then_inc(drop_id_set, 1)
                    nc.vector.tensor_copy(before[:], const[:, C_BEFORE:C_BEFORE + P]).then_inc(before_set, 1)
                    nc.vector.tensor_copy(base[:], const[0:1, C_BASE:C_BASE + E_N]).then_inc(before_set, 1)

            ties = ctx.enter_context(dve.register("ties"))
            run(step, -2, TILES + 2)(dve)
            dve.wait_ge(share_ready, TILES)
            combine(0)
            combine(1)

        @block.tensor
        def _(pe):
            def unit_rows(u, fronts):
                pe.wait_ge(xs_in[u.slot], u.uses * 16)
                pe.wait_ge(xs_ready, u.n + 2)
                pe.wait_ge(q_ready, fronts)
                nc.tensor.transpose(ps_xs, xs_ring[:, u.slot, :], ident).then_inc(xs_mm, 1)

            def unit_hidden(u):
                pe.wait_ge(w_in[u.slot], u.uses * 16)
                pe.wait_ge(h_ready, u.n + 3 - u.back)
                pe.wait_ge(xs_ready, u.n + 3)
                for c in range(FC):
                    last = nc.tensor.matmul(ps_h[u.bank][:, c, :], w_ring[:, u.slot, c * P:c * P + P],
                                            xs_t[:, u.par, :], start=True, stop=True)
                last.then_inc(h_mm, 1)

            def unit_out(u):
                pe.wait_ge(y_ready, u.n + 3 - u.back)
                pe.wait_ge(h_ready, u.n + 3)
                y = ps_y[u.bank]
                for c in range(FC):
                    nc.tensor.matmul(y, h_t[:, u.par, c, :], w_ring[:, u.slot, F + c * D:F + c * D + D],
                                     start=(c == 0), stop=False)
                nc.tensor.matmul(y, ones_row[:], w_ring[0:1, u.slot, 2 * F + FC:WW], start=False, stop=True).then_inc(y_mm, 1)

            def rank(k, kk, units):
                ch = chunk_of_router(k, kk)
                own = chosen[:, bass.ds(k - 2, 1), :].rearrange("p a e -> p (a e)")
                pe.wait_ge(chosen_ready, k - 1)
                if kk == 2:
                    pe.wait_ge(before_set, 2)
                    pe.wait_ge(seen_zero, 1)
                if later(kk, 2, 1):
                    pe.wait_ge(seen_ready, k - 2)
                early = kk == CT + 1
                pe.wait_ge(q_ready, (k + 3) if kk is None else min(kk + 3 - early, TILES))
                if units:
                    pe.wait_ge(xs_ready, units[-1].n + 3)
                if kk in (CT + 1, TILES + 1):
                    nc.tensor.matmul(ps_total, ones_bf[:], seen[:, ch, :], start=True, stop=False)
                    nc.tensor.matmul(ps_total, ones_bf[:], own, start=False, stop=True)
                nc.tensor.matmul(ps_rank, before[:], own, start=True, stop=False)
                nc.tensor.matmul(ps_rank, ones_bf[:], seen[:, ch, :], start=False, stop=False)
                nc.tensor.matmul(ps_rank, ones_bf[0:1, :], base[:], start=False, stop=True).then_inc(rank_mm, 1)

            def ranks_left(k, kk):
                if later(kk, 3, 0):
                    pe.wait_ge(rank_read, k - 2)

            def step(k, par, kk, half, units):
                nxt = (par + 1) % 2
                att, rou = has(kk, 1), has(kk, 2)
                att_batch, next_batch = (half - 1 + par, half + par) if kk is None else ((kk - 1) // 2, (kk + 1) // 2)
                fronts = k + 2 if kk is None else min(kk + 2, TILES)
                u = (units + [None, None])[:2]

                def scores(hh):
                    heads = slice(8 * hh, 8 * hh + 8)
                    mm = nc.tensor.matmul(ps_s[:, heads, :], q_t[:, nxt, :],
                                          kb[:, bass.ds(next_batch, 1), heads, :].rearrange("p a h n -> p (a h n)"),
                                          start=True, stop=True)
                    if hh == 1:
                        mm.then_inc(s_mm, 1)

                if u[0]:
                    ranks_left(k, kk)
                    unit_rows(u[0], fronts)
                if has(kk, -1):
                    pe.wait_ge(q_ready, k + 2)
                    pe.wait_ge(kb_ready, B if kk is None else next_batch + 1)
                    if later(kk, -1, 1):
                        pe.wait_ge(s_ready, k + 1)
                    scores(0)
                if rou:
                    pe.wait_ge(xn2_ready, k - 1)
                    pe.wait_ge(count_read, k if kk is None or kk <= TILES else TILES)
                    nc.tensor.transpose(ps_x2, xn2[:, par, :], ident).then_inc(x2_mm, 1)
                if has(kk, -1):
                    scores(1)
                if rou:
                    pe.wait_ge(x2_ready, k - 1)
                    nc.tensor.matmul(ps_l, xn2_t[:], wr[:], start=True, stop=True).then_inc(l_mm, 1)
                if kk == TILES + 1:
                    rank(k, kk, units)
                if att:
                    pe.wait_ge(drop_ok, k)
                    pe.wait_ge(z_ready, k)
                    if kk == 1:
                        pe.wait_ge(drop_id_set, 1)
                    if kk == 1:
                        pe.wait_ge(v_ready, 2)
                    if later(kk, 1, 1):
                        pe.wait_ge(pt_ready, k - 1)
                    for j in range(PAIRS):
                        nc.tensor.matmul(ps_p[:, j, :], z_sb[:, nxt, j, :], ident, start=True, stop=False, is_transpose=True)
                        last = nc.tensor.matmul(ps_p[:, j, :], drop[:, nxt, 2 * j:2 * j + 2, :].rearrange("p h n -> p (h n)"),
                                                drop_id[:], start=False, stop=True)
                    last.then_inc(p_mm, 1)
                if u[0]:
                    unit_hidden(u[0])
                if kk == CT + 1:
                    ranks_left(k, kk)
                    rank(k, kk, units)
                if att:
                    pe.wait_ge(pt_ready, k)
                    if later(kk, 1, 1):
                        pe.wait_ge(idx_ready, k - 1)
                    for j in range(PAIRS):
                        last = nc.tensor.matmul(ps_pv[:, j, :], p_t[:, j, :],
                                                vb[:, bass.ds(att_batch, 1), j, :].rearrange("p a v -> p (a v)"),
                                                start=True, stop=True)
                    last.then_inc(pv_mm, 1)
                if u[1]:
                    unit_rows(u[1], fronts)
                if u[0]:
                    unit_out(u[0])
                if u[1]:
                    unit_hidden(u[1])
                if att:
                    pe.wait_ge(cn_ready, k)
                    nc.tensor.transpose(ps_c, cn[:], ident).then_inc(c_mm, 1)
                if att:
                    pe.wait_ge(ct_ready, k)
                    if kk == 1:
                        pe.wait_ge(w_late, 64)
                    nc.tensor.matmul(ps_o, c_t[:], wo[:], start=True, stop=False)
                    nc.tensor.matmul(ps_o, ones_row[:], bo_row[:], start=False, stop=True).then_inc(o_mm, 1)
                if has(kk, -2):
                    pe.wait_ge(xn_ready, k + 3)
                    if later(kk, -2, 1):
                        pe.wait_ge(q_ready, k + 2)
                    if units:
                        pe.wait_ge(xs_ready, units[-1].n + 3)
                    if not units and kk != CT + 1:
                        ranks_left(k, kk)
                    if kk == CT + 1:
                        pe.wait_ge(rank_read, k - 1)
                        pe.wait_ge(total_read, 1)
                    nc.tensor.transpose(ps_xt, xn[:, par, :], ident).then_inc(xt_mm, 1)
                if has(kk, -2):
                    pe.wait_ge(xt_ready, k + 3)
                    if kk == -2:
                        pe.wait_ge(w_q, 32)
                    nc.tensor.matmul(ps_q, wq[:], xn_t[:, par, :], start=True, stop=True).then_inc(q_mm, 1)
                if u[1]:
                    unit_out(u[1])
                if rou and kk not in (CT + 1, TILES + 1):
                    rank(k, kk, units)
                if has(kk, 0):
                    pe.wait_ge(drop_ready, k + 1)
                    if att:
                        pe.wait_ge(x1_ready, k)
                    nc.tensor.matmul(ps_count[:, 0:1], count[:, 2:3], ones_col[:], start=True, stop=True)
                    nc.tensor.matmul(ps_count[:, 1:2], count[:, 0:1], removed_weight[:], start=True, stop=False)
                    nc.tensor.matmul(ps_count[:, 1:2], count[:, 1:2], removed_weight[:], start=False, stop=True).then_inc(count_mm, 1)

                if kk == -1:
                    pe.wait_ge(w_v, 48)
                    pe.wait_ge(consts_set, 7)
                    for b in range(B):
                        nc.tensor.matmul(ps_p[:, b, :], ctx_twice[:, b].rearrange("p a n -> p (a n)"), wv[:], start=True, stop=False)
                        last = nc.tensor.matmul(ps_p[:, b, :], ones_row[:], bv_row[:], start=False, stop=True)
                    last.then_inc(v_mm, 1)

            pe.sem_inc(h_mm, 2)
            pe.sem_inc(y_mm, 2)
            pe.wait_ge(w_kv, 48)
            nc.tensor.matmul(ps_s[:, 0:8, :], wk[:], ctx_t[:], start=True, stop=True).then_inc(k_mm, 1)
            pe.wait_ge(consts_in, 16)
            run(step, -2, TILES + 2)(pe)

            pe.wait_ge(rank_read, TILES)
            pe.wait_ge(total_read, CHUNKS)
            units_after(pe, lambda u: unit_rows(u, TILES), unit_hidden, unit_out)


def kernel(**inputs):
    import concourse.bacc as bacc
    from concourse.bass_utils import run_bass_kernel_spmd
    a = {n: np.asarray(v) for n, v in inputs.items()}
    L = "L0_xattn_"
    M = "L0_ffn_"
    const = np.zeros((P, C_W), np.float32)
    const[:, C_ID:C_ID + P] = np.eye(P, dtype=np.float32)
    const[np.arange(P), C_HM + np.arange(P) // HD] = 1.0
    const[:, C_IOTA:C_IOTA + E_N] = np.arange(E_N, dtype=np.float32)
    const[:, C_EDGE:C_EDGE + CT] = P * np.arange(CT)
    const[:, C_UPTO:C_UPTO + E_N * E_N] = np.tril(np.ones((E_N, E_N))).ravel()
    const[:, C_UNIT:C_UNIT + UNITS] = np.arange(UNITS)
    const[:, C_BASE:C_BASE + E_N] = P * CT * np.arange(E_N)
    const[:, C_BEFORE:C_BEFORE + P] = np.triu(np.ones((P, P)), 1)
    c = a["ctx_1024"].transpose(2, 0, 1)
    arrays = {
        "x": a["x"].reshape(TILES, P, D).transpose(1, 0, 2),
        "const": const,
        "wq": a[L + "Wq"].T, "wk": a[L + "Wk"].T, "wv": a[L + "Wv"].T, "wo": a[L + "Wo"].T,
        "bq": a[L + "bq"].reshape(P, 1), "bk": a[L + "bk"].reshape(P, 1),
        "bv": a[L + "bv"].reshape(1, D), "bo": a[L + "bo"].reshape(1, D),
        "ctx": c,
        "gates": np.broadcast_to(np.concatenate([a["g_xattn"], a["g_ffn"]])[None, :], (P, 2)),
        "wr": a[M + "w_router"],
        "w": np.concatenate([
            a[M + "w1"],
            a[M + "w2"].reshape(E_N, FC, P, D).transpose(0, 2, 1, 3).reshape(E_N, P, F),
            a[M + "b1"].reshape(E_N, FC, P).transpose(0, 2, 1),
            np.broadcast_to(a[M + "b2"][:, None, :], (E_N, P, D)),
        ], axis=2),
    }
    nc = bacc.Bacc("TRN2", target_bir_lowering=False, num_devices=1)
    t, feed = {}, {}
    for n, v in arrays.items():
        v = np.ascontiguousarray(v)
        feed["in_" + n] = v
        t[n] = nc.dram_tensor("in_" + n, v.shape, F32, kind="ExternalInput").ap()
    out = nc.dram_tensor("out", (TILES, P, D), F32, kind="ExternalOutput").ap()
    t["out"] = out.rearrange("t p d -> p t d")
    for n, blocks in (("xs", BLOCKS), ("ys", UNITS)):
        t[n] = [nc.dram_tensor(f"{n}{ch}", (blocks * P, D), F32, kind="Internal").ap() for ch in range(CHUNKS)]
    build(nc, t)
    r = run_bass_kernel_spmd(nc, [feed], core_ids=[0])
    return r.results[0]["out"].reshape(B, S, D)
```
